# Optimizing a Trainium2 kernel written in Bass

```python
import numpy as np
import jax
import jax.numpy as jnp

def _softmax(x, axis=-1):
    return jax.nn.softmax(x, axis=axis)

def _gelu(x):
    return jax.nn.gelu(x, approximate=True)

def _silu(x):
    return jax.nn.silu(x)

def _sigmoid(x):
    return jax.nn.sigmoid(x)

def _layernorm(x, axis=-1, eps=1e-05):
    m = jnp.mean(x, axis=axis, keepdims=True)
    v = jnp.var(x, axis=axis, keepdims=True)
    return (x - m) / jnp.sqrt(v + eps)

def _scatter_add(tgt, idx, src, axis=0):
    return tgt.at[idx].add(src)

def _segment_sum(src, seg, n):
    return jax.ops.segment_sum(src, seg, n)
kernel_name = 'mk_xattn_ffn_d1_seqx_r4_12f050'

def setup_inputs(seed: int=0):
    np.random.seed(seed)
    _w = jnp.asarray

    def _rec_inputs():
        import jax
        import jax.numpy as jnp
        _rk = jax.random.key(seed)
        x = 0.000341 + 1 * jax.random.normal(jax.random.fold_in(_rk, 1), (8, 256, 512), jnp.float32)
        _lenS = 256 - jax.random.randint(jax.random.fold_in(_rk, 7), (8,), 0, max(1, 256 // 4) + 1, jnp.int32)
        _lenS2 = 256 - jax.random.randint(jax.random.fold_in(_rk, 8), (8,), 0, max(1, 256 // 4) + 1, jnp.int32)
        _ctx_2048P = jax.random.normal(jax.random.fold_in(_rk, 11), (8, 16, 512), jnp.float32)
        _ctx_2048c = jax.random.dirichlet(jax.random.fold_in(_rk, 511), 0.3 * jnp.ones((16,), jnp.float32), (8, 256))
        _ctx_2048t = jnp.einsum('bsk,bkd->bsd', _ctx_2048c, _ctx_2048P)
        _ctx_2048t = _ctx_2048t * jax.lax.rsqrt(jnp.mean(jnp.square(_ctx_2048t)) + 1e-12) * 0.953939
        ctx_2048 = -1.47943e-05 + 1.00017 * (_ctx_2048t + 0.3 * jax.random.normal(jax.random.fold_in(_rk, 611), (8, 256, 512), jnp.float32))
        return (x, ctx_2048)
    x, ctx_2048 = _rec_inputs()

    def _L0_xattn_setup():
        import jax, jax.numpy as jnp
        import numpy as np

        def _wkv(time_decay, time_first, k, v):
            w = -jnp.exp(time_decay)
            u = time_first
            B, T, C = k.shape
            aa = jnp.zeros((B, C), dtype=k.dtype)
            bb = jnp.zeros((B, C), dtype=k.dtype)
            pp = jnp.full((B, C), -1e+38, dtype=k.dtype)

            def step(carry, kv_t):
                aa, bb, pp = carry
                kt, vt = kv_t
                ww = u + kt
                q = jnp.maximum(pp, ww)
                e1 = jnp.exp(pp - q)
                e2 = jnp.exp(ww - q)
                y_t = (e1 * aa + e2 * vt) / (e1 * bb + e2)
                ww2 = pp + w
                q2 = jnp.maximum(ww2, kt)
                e1b = jnp.exp(ww2 - q2)
                e2b = jnp.exp(kt - q2)
                new_carry = (e1b * aa + e2b * vt, e1b * bb + e2b, q2)
                return (new_carry, y_t)
            ks = jnp.transpose(k, (1, 0, 2))
            vs = jnp.transpose(v, (1, 0, 2))
            _, ys = jax.lax.scan(step, (aa, bb, pp), (ks, vs))
            return jnp.transpose(ys, (1, 0, 2))
        key = jax.random.key(seed)
        k1, k2, k3, k4 = jax.random.split(key, 4)
        B, T, C = (8, 256, 512)
        return {'batch_size': B, 'seq_len': T, 'embedding_dim': C, 'time_decay': jax.random.normal(k1, (C,), dtype=jnp.float32), 'time_first': jax.random.normal(k2, (C,), dtype=jnp.float32), 'k': jax.random.normal(k3, (B, T, C), dtype=jnp.float32), 'v': jax.random.normal(k4, (B, T, C), dtype=jnp.float32)}
    _L0_xattn_all = _L0_xattn_setup()
    _L0_xattn_in = {k: v for k, v in _L0_xattn_all.items() if k in ('time_decay', 'time_first')}
    del _L0_xattn_all

    def _L0_ffn_setup():
        import jax, jax.numpy as jnp
        import numpy as np
        TOP_K = 2
        key = jax.random.key(seed)
        ks = jax.random.split(key, 5)
        B, S, D, M, E = (4, 512, 512, 512, 8)
        x = jax.random.normal(ks[0], (B, S, D), dtype=jnp.float32)
        gate_kernel = jax.random.normal(ks[1], (D, E), dtype=jnp.float32) / np.sqrt(D)
        wi_0 = jax.random.normal(ks[2], (E, D, M), dtype=jnp.float32) / np.sqrt(D)
        wi_1 = jax.random.normal(ks[3], (E, D, M), dtype=jnp.float32) / np.sqrt(D)
        wo = jax.random.normal(ks[4], (E, M, D), dtype=jnp.float32) / np.sqrt(M)
        return {'x': x, 'gate_kernel': gate_kernel, 'wi_0': wi_0, 'wi_1': wi_1, 'wo': wo}
    _L0_ffn_all = _L0_ffn_setup()
    _L0_ffn_in = {k: v for k, v in _L0_ffn_all.items() if k in ('gate_kernel', 'wi_0', 'wi_1', 'wo')}
    del _L0_ffn_all
    return {'x': x, 'ctx_2048': ctx_2048, 'L0_xattn_time_decay': _L0_xattn_in['time_decay'], 'L0_xattn_time_first': _L0_xattn_in['time_first'], 'L0_ffn_gate_kernel': _L0_ffn_in['gate_kernel'], 'L0_ffn_wi_0': _L0_ffn_in['wi_0'], 'L0_ffn_wi_1': _L0_ffn_in['wi_1'], 'L0_ffn_wo': _L0_ffn_in['wo']}

def reference(x, ctx_2048, L0_xattn_time_decay, L0_xattn_time_first, L0_ffn_gate_kernel, L0_ffn_wi_0, L0_ffn_wi_1, L0_ffn_wo):
    import jax
    import jax.numpy as jnp

    def _L0_xattn_ref(batch_size, seq_len, embedding_dim, time_decay, time_first, k, v):
        import jax, jax.numpy as jnp
        import numpy as np

        def _wkv(time_decay, time_first, k, v):
            w = -jnp.exp(time_decay)
            u = time_first
            B, T, C = k.shape
            aa = jnp.zeros((B, C), dtype=k.dtype)
            bb = jnp.zeros((B, C), dtype=k.dtype)
            pp = jnp.full((B, C), -1e+38, dtype=k.dtype)

            def step(carry, kv_t):
                aa, bb, pp = carry
                kt, vt = kv_t
                ww = u + kt
                q = jnp.maximum(pp, ww)
                e1 = jnp.exp(pp - q)
                e2 = jnp.exp(ww - q)
                y_t = (e1 * aa + e2 * vt) / (e1 * bb + e2)
                ww2 = pp + w
                q2 = jnp.maximum(ww2, kt)
                e1b = jnp.exp(ww2 - q2)
                e2b = jnp.exp(kt - q2)
                new_carry = (e1b * aa + e2b * vt, e1b * bb + e2b, q2)
                return (new_carry, y_t)
            ks = jnp.transpose(k, (1, 0, 2))
            vs = jnp.transpose(v, (1, 0, 2))
            _, ys = jax.lax.scan(step, (aa, bb, pp), (ks, vs))
            return jnp.transpose(ys, (1, 0, 2))
        assert seq_len <= 256
        return _wkv(time_decay, time_first, k, v)

    def _L0_ffn_ref(x, gate_kernel, wi_0, wi_1, wo):
        import jax, jax.numpy as jnp
        import numpy as np
        TOP_K = 2
        E = gate_kernel.shape[-1]
        gate_logits = jnp.einsum('bsd,de->bse', x, gate_kernel)
        top_k_weights, top_k_indices = jax.lax.top_k(gate_logits, TOP_K)
        top_k_weights = jax.nn.softmax(top_k_weights.astype(jnp.float32), axis=-1).astype(x.dtype)
        combine_w = jnp.sum(jax.nn.one_hot(top_k_indices, E, dtype=x.dtype) * top_k_weights[..., None], axis=-2)
        h0 = jnp.einsum('bsd,edm->bsem', x, wi_0)
        h1 = jnp.einsum('bsd,edm->bsem', x, wi_1)
        h = jax.nn.silu(h0) * h1 * combine_w[..., None]
        out = jnp.einsum('bsem,emd->bsd', h, wo)
        return out
    x = x + _L0_xattn_ref(8, 256, 512, L0_xattn_time_decay, L0_xattn_time_first, _layernorm(x, axis=-1), ctx_2048)
    x = x + _L0_ffn_ref(_layernorm(x, axis=-1), L0_ffn_gate_kernel, L0_ffn_wi_0, L0_ffn_wi_1, L0_ffn_wo)
    return x

_drawn_inputs = setup_inputs


def setup_inputs(seed=0):
    import zlib

    import numpy as np

    out = dict(_drawn_inputs(seed))
    spreads = {}
    factors = {}
    for name, (base, spread) in spreads.items():
        noise = np.random.default_rng([zlib.crc32(name.encode()), seed]).standard_normal(out[name].shape)
        drawn = base * np.exp(spread * noise) if base else spread * noise
        out[name] = jnp.asarray(drawn.astype(out[name].dtype))
    for name, factor in factors.items():
        out[name] = (out[name] * factor).astype(out[name].dtype)
    return out
```

```python
from contextlib import ExitStack

import concourse.bass as bass
from concourse import mybir

P = 128
B, T, C = 8, 256, 512
NTOK = B * T
NT = NTOK // P
NC = C // P
GT = 4
NG = NT // GT
GW = GT * P
EX, M = 8, 512
NK = C // P
EPS = 1e-5
CT = 5
CAP = CT * P
HW = CAP // 2
JT = NT
OOB = NTOK
OV = max(n * min(JT - CT, JT) if 2 * n <= 4 else (2 * NTOK + n * (P - 1)) // P - CT * n
         for n in range(1, EX + 1) if n <= 2 or (2 * NTOK + n * (P - 1)) // P - CT * n > 0)

F32, F32R = mybir.dt.float32, mybir.dt.float32r
BF16, I32, U32 = mybir.dt.bfloat16, mybir.dt.int32, mybir.dt.uint32
ALU, ACT, AX = mybir.AluOpType, mybir.ActivationFunctionType, mybir.AxisListType


def build(nc, x, ctx, decay, first, gate, wi0, wi1, wo, out):
    weights = [w.rearrange("e (k p) m -> e p k m", p=P) for w in (wi0, wi1, wo)]
    x_in = x.rearrange("b (h p) c -> p (b h) c", p=P)
    v_in = ctx.rearrange("b (h p) c -> p (b h) c", p=P)
    out_rows = out.rearrange("b t c -> (b t) c")
    xn_rows = nc.dram_tensor("xn_rows", [NTOK, C], F32, kind="Internal").ap()
    table = nc.dram_tensor("table", [EX * NTOK, 2], I32, kind="Internal").ap()

    with ExitStack() as keep:
        def sb(name, shape, dt=F32, stack=keep):
            return stack.enter_context(nc.sbuf_tensor(name, shape, dt))

        def sem(name):
            return keep.enter_context(nc.semaphore(name))

        raw = sb("raw", [P, 3, NK, M])
        wh = [sb("wh0", [P, 3, NK, M], F32R), None]
        wl = [sb("wl0", [P, 3, NK, M], F32R), None]
        ident = sb("ident", [P, P])
        before = sb("before", [P, P], BF16)
        ones = sb("ones", [P, P], BF16)
        lists = sb("lists", [P, EX * JT + 1, 2], I32)
        totals = sb("totals", [P, EX])
        tiles_over = sb("tiles_over", [P, 1], I32)
        over_expert = sb("over_expert", [P, OV], I32)
        over_column = sb("over_column", [P, OV], I32)
        over_iota = sb("over_iota", [P, OV])
        ones8 = sb("ones8", [P, EX])
        cnt_b = sb("cnt_b", [P, EX], I32); cnt_t = sb("cnt_t", [P, EX], I32)
        cnt_f = sb("cnt_f", [P, EX]); extra = sb("extra", [P, EX]); extra_sum = sb("extra_sum", [P, EX])
        past = sb("past", [P, OV, EX]); past_n = sb("past_n", [P, OV, EX])
        past_experts = sb("past_experts", [P, OV]); past_tiles = sb("past_tiles", [P, OV])
        over_j = sb("over_j", [P, OV]); over_c = sb("over_c", [P, OV]); over_d = sb("over_d", [P, OV])

        phase_a = ExitStack()
        def sa(name, shape, dt=F32):
            return sb(name, shape, dt, phase_a)
        X = sa("X", [P, NT, C])
        K = sa("K", [P, GT, C])
        V = sa("V", [P, GT, C])
        decay_row = sa("decay_row", [P, NC, GW])
        f1 = sa("f1", [P, 2, GW])
        f2 = sa("f2", [P, 4, GW])
        vs = sa("vs", [P, 2, GW])
        g1 = sa("g1", [P, 2, GW])
        g2 = sa("g2", [P, 2, GW])
        st_a = sa("st_a", [P, 2, GW])
        st_b = sa("st_b", [P, 2, GW])
        Y = sa("Y", [P, NC, GW])
        XN = sa("XN", [P, GT, C])
        XNT = sa("XNT", [P, 2, NC, P])
        stat1 = sa("stat1", [P, NT, 6])
        mv1 = sa("mv1", [P, NT, 2])
        stat2 = sa("stat2", [P, GT, 6])
        mv2 = sa("mv2", [P, GT, 2])
        ve = sa("ve", [P, NT]); r0 = sa("r0", [P, NT]); na = sa("na", [P, NT]); nb = sa("nb", [P, NT])
        ncf = sa("ncf", [P, NT]); rs1 = sa("rs1", [P, NT]); nm1 = sa("nm1", [P, NT])
        ve2 = sa("ve2", [P, GT]); q0 = sa("q0", [P, GT]); qa = sa("qa", [P, GT]); qb = sa("qb", [P, GT])
        qc = sa("qc", [P, GT]); rs2 = sa("rs2", [P, GT]); lnv = sa("lnv", [P, NT]); lnv2 = sa("lnv2", [P, GT])
        td = sa("td", [P, NC]); tf = sa("tf", [P, NC]); etd = sa("etd", [P, NC]); dd = sa("dd", [P, NC])
        ub1 = sa("ub1", [P, NC]); ub2 = sa("ub2", [P, NC])
        gk = sa("gk", [P, NC, EX])
        iota8 = sa("iota8", [P, EX])
        tok = sa("tok", [P, NT], I32)
        lg = sa("lg", [P, GT, EX]); m8 = sa("m8", [P, GT, 8]); i8 = sa("i8", [P, GT, 8], U32)
        idxf = sa("idxf", [P, GT, 2]); dlt = sa("dlt", [P, GT]); e2 = sa("e2", [P, GT])
        e2p = sa("e2p", [P, GT]); p1 = sa("p1", [P, GT])
        oh = sa("oh", [P, GT, 2, EX]); ohr = sa("ohr", [P, GT, 2, EX])
        msk = sa("msk", [P, GT, EX], BF16)
        cum = sa("cum", [P, GT + 1, EX], BF16)
        rk = sa("rk", [P, GT, 2]); rki = sa("rki", [P, GT, 2], I32); lo7 = sa("lo7", [P, GT, 2], I32)
        hi4 = sa("hi4", [P, GT, 2], I32); ebs = sa("ebs", [P, GT, 2], I32); lh = sa("lh", [P, GT, 2], I32)
        row = sa("row", [P, GT, 2], I32)
        rec = sa("rec", [P, GT, 2, 2], I32)
        blank = sa("blank", [P, P, 2], I32)
        phase_a.close()

        phase_b = ExitStack()
        def sbb(name, shape, dt=F32):
            return sb(name, shape, dt, phase_b)
        wh[1] = sbb("wh1", [P, 3, NK, M], F32R)
        wl[1] = sbb("wl1", [P, 3, NK, M], F32R)
        xg = sbb("xg", [P, 2, C])
        xth = [sbb(f"xth{i}", [P, NK, CAP], F32R) for i in range(2)]
        xtl = [sbb(f"xtl{i}", [P, NK, CAP], F32R) for i in range(2)]
        hth = sbb("hth", [P, NK, CAP], F32R)
        htl = sbb("htl", [P, NK, CAP], F32R)
        sl = sbb("sl", [P, 2, HW])
        hm = sbb("hm", [P, 2, HW])
        acc = sbb("acc", [P, CT, C])
        idx = sbb("idx", [P, 2, CT], I32)
        phase_b.close()

        phase_c = ExitStack()
        def sc(name, shape, dt=F32):
            return sb(name, shape, dt, phase_c)
        o_idx = sc("o_idx", [P, 2], I32)
        o_x = sc("o_x", [P, C]); o_acc = sc("o_acc", [P, C]); o_xt = sc("o_xt", [P, NK, P])
        o_s = sc("o_s", [P, M]); o_h = sc("o_h", [P, M]); o_ht = sc("o_ht", [P, NK, P]); o_r = sc("o_r", [P, C])
        phase_c.close()

        bank = [keep.enter_context(nc.psum_tensor(f"bank{i}", [P, 512], F32)) for i in range(8)]
        logits = bank[7][:, 0:GT * EX].rearrange("p (j e) -> p j e", e=EX)
        ranks = bank[7][:, 64:64 + GT * EX].rearrange("p (j e) -> p j e", e=EX)

        x_loaded = [sem(f"x_loaded{g}") for g in range(NG)]
        small_loaded = sem("small_loaded")
        v_loaded = sem("v_loaded")
        blank_made = sem("blank_made"); table_blank = sem("table_blank")
        const_made = sem("const_made"); ident_made = sem("ident_made")
        decay_exp = sem("decay_exp"); dve_prologue = sem("dve_prologue")
        ln1 = sem("ln1"); ln1_act = sem("ln1_act")
        k_ready = sem("k_ready")
        k_turned = sem("k_turned")
        v_turned = sem("v_turned")
        f2_made = sem("f2_made")
        vs_made = sem("vs_made")
        b_scanned = sem("b_scanned")
        g1_made = sem("g1_made")
        a_scanned = sem("a_scanned")
        den_made = sem("den_made")
        g2_made = sem("g2_made")
        num_made = sem("num_made")
        y_made = sem("y_made")
        ln_made = sem("ln_made"); rden_made = sem("rden_made")
        y_turned = sem("y_turned")
        x1_made = sem("x1_made")
        x1_stored = sem("x1_stored")
        xn_stored = [sem(f"xn_stored{j}") for j in range(GT)]
        xn_free = sem("xn_free")
        ln2 = sem("ln2"); ln2_act = sem("ln2_act")
        stat2_made = sem("stat2_made"); mv2_made = sem("mv2_made")
        xn_made = sem("xn_made")
        xn_turned = sem("xn_turned")
        xnt_made = sem("xnt_made")
        gated = sem("gated")
        route = sem("route")
        mask_made = sem("mask_made"); delta_made = sem("delta_made"); e2_made = sem("e2_made")
        ranked = sem("ranked")
        ranks_read = sem("ranks_read")
        rows_made = sem("rows_made")
        rec_stored = sem("rec_stored")
        row_init = sem("row_init")
        totals_made = sem("totals_made")
        raw_loaded = [sem(f"raw_loaded{m}") for m in range(3)]
        wh_made = sem("wh_made"); wl_made = sem("wl_made")
        lists_loaded = sem("lists_loaded")
        phase_a_done = sem("phase_a_done")
        b_cleared = sem("b_cleared")
        idx_made = sem("idx_made")
        xg_loaded = [sem(f"xg_loaded{i}") for i in range(2)]
        xg_turned = sem("xg_turned")
        xh_made = sem("xh_made")
        xl_made = sem("xl_made")
        h0_done = sem("h0_done"); h1_done = sem("h1_done")
        silu_made = sem("silu_made")
        hm_made = sem("hm_made")
        hh_made = sem("hh_made"); hl_made = sem("hl_made")
        out_done = sem("out_done")
        fin_made = sem("fin_made")
        acc_loaded = [sem(f"acc_loaded{j}") for j in range(CT)]
        acc_stored = [sem(f"acc_stored{j}") for j in range(CT)]
        over_made = sem("over_made"); over_ready = sem("over_ready")
        o_w = sem("o_w"); o_copied = sem("o_copied"); o_xin = sem("o_xin"); o_ain = sem("o_ain")
        o_xturn = sem("o_xturn"); o_xtm = sem("o_xtm"); o_h01 = sem("o_h01"); o_sm = sem("o_sm")
        o_hm = sem("o_hm"); o_hturn = sem("o_hturn"); o_htm = sem("o_htm"); o_out = sem("o_out")
        o_fin = sem("o_fin"); o_sto = sem("o_sto")

        waits_ended = sem("waits_ended")
        LN1_STEPS = 4
        ROUTE_STEPS = 21

        def apart(engine):
            engine.sem_inc(waits_ended, 1)

        block = keep.enter_context(nc.Block())

        @block.sync
        def _(sp):
            sp.dma_start(X[:, 0:GT, :], x_in[:, 0:GT, :]).then_inc(x_loaded[0], 16)
            sp.dma_start(td[:, :], decay).then_inc(small_loaded, 16)
            sp.dma_start(tf[:, :], first).then_inc(small_loaded, 16)
            sp.dma_start(gk[:, :, :], gate).then_inc(small_loaded, 16)
            for g in range(1, NG):
                sp.dma_start(X[:, g * GT:(g + 1) * GT, :], x_in[:, g * GT:(g + 1) * GT, :]).then_inc(x_loaded[g], 16)
                if g == 1:
                    sp.dma_start(V[:, :, :], v_in[:, 0:GT, :]).then_inc(v_loaded, 16)
            sp.wait_ge(blank_made, 2)
            sp.dma_start(table.rearrange("(p n) w -> p n w", p=P), blank[:, :, :]).then_inc(table_blank, 16)
            for m in range(3):
                sp.dma_start(raw[:, m, :, :], weights[m][0]).then_inc(raw_loaded[m], 16)
            with sp.Fori(1, NG) as s:
                sp.wait_ge(v_turned, s * NC)
                sp.dma_start(V[:, :, :], v_in[:, bass.ds(s * GT, GT), :]).then_inc(v_loaded, 16)
            sp.wait_ge(rec_stored, 16 * 2 * GT * (NG + 1))
            sp.dma_start(lists[:, 0:EX * JT, :].rearrange("p (e j) w -> p e (j w)", e=EX),
                         table.rearrange("(e p j) w -> p e (j w)", e=EX, p=P)).then_inc(lists_loaded, 16)
            with sp.Fori(1, EX) as e:
                for m in range(3):
                    sp.wait_ge(wl_made, (e - 1) * 3 * NK + NK * (m + 1))
                    sp.dma_start(raw[:, m, :, :], weights[m][e]).then_inc(raw_loaded[m], 16)
            sp.wait_ge(over_ready, 1)
            over = sp.value_load(tiles_over[0:1, 0:1], min_val=0, max_val=OV)
            with sp.If(over > 0):
                with sp.Fori(0, OV) as k:
                    sp.wait_ge(o_fin, k + 1)
                    e = sp.value_load(over_expert[0:1, bass.ds(k, 1)], min_val=0, max_val=EX - 1)
                    for m in range(3):
                        sp.dma_start(raw[:, m, :, :], weights[m][e]).then_inc(o_w, 16)

        @block.gpsimd
        def _(pool):
            for s_, n in ((k_turned, 1), (f2_made, 2), (vs_made, 2), (b_scanned, 2), (den_made, 2),
                          (g2_made, 2), (y_made, 4), (y_turned, 1), (x1_made, 2), (xnt_made, 1), (xn_free, 1),
                          (gated, 2), (ranks_read, 1), (xg_turned, 2), (xl_made, 2), (silu_made, 2),
                          (hm_made, 2), (out_done, 1), (fin_made, 2), (o_fin, 1)):
                pool.sem_inc(s_, n)
            pool.memset(ident[:, :], 0.0).then_inc(ident_made, 1)
            pool.wait_ge(ident_made, 1)
            pool.affine_select(out=ident[:, :], in_=ident[:, :], compare_op=ALU.not_equal, fill=1.0, base=0,
                               pattern=[[-1, P]], channel_multiplier=1).then_inc(ident_made, 1)
            pool.memset(before[:, :], 1.0).then_inc(const_made, 1)
            pool.memset(ones[:, :], 1.0)
            pool.memset(blank[:, :, 0], OOB).then_inc(blank_made, 1)
            pool.memset(blank[:, :, 1], 0).then_inc(blank_made, 1)
            pool.memset(lists[:, EX * JT, 0:1], OOB)
            pool.memset(lists[:, EX * JT, 1:2], 0)
            pool.memset(row[:, :, :], EX * NTOK).then_inc(row_init, 1)
            pool.memset(rec[:, :, :, :], 0).then_inc(row_init, 1)
            pool.memset(cum[:, 0, :], 0.0)
            pool.iota(tok[:, :], [[P, NT]], base=0, channel_multiplier=1)
            pool.iota(over_iota[:, :], [[1, OV]], base=0, channel_multiplier=0, allow_small_or_imprecise_dtypes=True)
            pool.memset(ones8[:, :], 1.0)
            pool.iota(iota8[:, :], [[1, EX]], base=0, channel_multiplier=0, allow_small_or_imprecise_dtypes=True)
            pool.wait_ge(const_made, 1)
            pool.affine_select(out=before[:, :], in_=before[:, :], compare_op=ALU.is_gt, fill=0.0, base=0,
                               pattern=[[1, P]], channel_multiplier=-1).then_inc(const_made, 1)
            pool.wait_ge(table_blank, 16)

            def store_entries(n):
                for i in n:
                    j, c = i // 2, i % 2
                    pool.indirect_dma_start(table, bass.IndirectOffsetOnAxis(ap=row[:, j, c:c + 1], axis=0),
                                            rec[:, j, c, :], None, bounds_check=last_entry,
                                            oob_is_err=False).then_inc(rec_stored, 16)

            last_entry, last_token = pool.to_reg(EX * NTOK - 1), pool.to_reg(NTOK - 1)
            with pool.Fori(0, NG) as s:
                for c in range(NC):
                    un = s * NC + c
                    vb, fb, gb = vs[:, c % 2, :], f2[:, c, :], g2[:, c % 2, :]
                    pool.wait_ge(vs_made, un + 3)
                    if c == 0:
                        pool.wait_ge(y_turned, s * GT + 1)
                    apart(pool)
                    pool.tensor_copy(Y[:, c, 0:GW:T], vb[:, 0:GW:T])
                    pool.wait_ge(f2_made, un + 3)
                    pool.wait_ge(y_made, un + 3)
                    pool.tensor_tensor(gb, fb, vb, ALU.mult).then_inc(g2_made, 1)
                    pool.wait_ge(b_scanned, un + 3)
                    fv = fb.rearrange("p (b t) -> p b t", t=T)[:, :, 1:T]
                    sv = st_b[:, c % 2, :].rearrange("p (b t) -> p b t", t=T)[:, :, 1:T]
                    pool.wait_ge(g2_made, un + 3)
                    pool.tensor_tensor(fv, fv, sv, ALU.add).then_inc(den_made, 1)
                    if c == 0:
                        pool.wait_ge(row_init, 2)
                        pool.wait_ge(rows_made, s + 1)
                        apart(pool)
                    store_entries((2 * c, 2 * c + 1))
            pool.wait_ge(rows_made, NG + 1)
            apart(pool)
            store_entries(range(2 * GT))

            pool.wait_ge(phase_a_done, 3)
            for j in range(GT):
                pool.wait_ge(xn_stored[j], 16 * NG)
            pool.wait_ge(x1_stored, 16 * NT)
            pool.memset(xg[:, :, :], 0.0).then_inc(b_cleared, 1)
            pool.memset(acc[:, :, :], 0.0).then_inc(b_cleared, 1)
            pool.wait_ge(b_cleared, 2)
            apart(pool)
            for j in range(CT):
                pool.indirect_dma_start(out_rows, bass.IndirectOffsetOnAxis(ap=lists[:, EX * JT, 0:1], axis=0),
                                        acc[:, j, :], None, bounds_check=last_token,
                                        oob_is_err=False).then_inc(acc_stored[j], 16)
            pool.wait_ge(lists_loaded, 16)
            lists_e = lists[:, 0:EX * JT, :].rearrange("p (e j) w -> p e j w", e=EX)

            def gather_x(p, i):
                r, j = i // CT, i % CT
                if j == 0:
                    pool.tensor_copy(idx[:, r, :], lists_e[:, p * 2 + r, 0:CT, 0]).then_inc(idx_made, 1)
                    pool.wait_ge(idx_made, p * 2 + r + 1)
                pool.wait_ge(xg_turned, p * 2 * CT + i + 1)
                apart(pool)
                pool.indirect_dma_start(xg[:, i % 2, :], None, xn_rows,
                                        bass.IndirectOffsetOnAxis(ap=idx[:, r, j:j + 1], axis=0),
                                        bounds_check=last_token, oob_is_err=False).then_inc(xg_loaded[i % 2], 16)

            def expert(p, r, last):
                e = p * 2 + r
                nxt = [(p, CT + j) if r == 0 else (p + 1, j) for j in range(CT)]
                for j in range(CT):
                    pool.wait_ge(acc_stored[j], (e + 1) * 16)
                apart(pool)
                if not last:
                    gather_x(*nxt[0]); gather_x(*nxt[1])
                for j in range(CT):
                    pool.indirect_dma_start(acc[:, j, :], None, out_rows,
                                            bass.IndirectOffsetOnAxis(ap=idx[:, r, j:j + 1], axis=0),
                                            bounds_check=last_token, oob_is_err=False).then_inc(acc_loaded[j], 16)
                if not last:
                    for j in range(2, CT):
                        gather_x(*nxt[j])
                for j in range(CT):
                    pool.wait_ge(fin_made, e * CT + j + 3)
                    apart(pool)
                    pool.indirect_dma_start(out_rows, bass.IndirectOffsetOnAxis(ap=idx[:, r, j:j + 1], axis=0),
                                            acc[:, j, :], None, bounds_check=last_token,
                                            oob_is_err=False).then_inc(acc_stored[j], 16)

            for j in range(CT):
                gather_x(0, j)
            with pool.Fori(0, EX // 2 - 1) as p:
                expert(p, 0, False)
                expert(p, 1, False)
            expert(EX // 2 - 1, 0, False)
            expert(EX // 2 - 1, 1, True)
            for j in range(CT):
                pool.wait_ge(acc_stored[j], (EX + 1) * 16)

            pool.wait_ge(over_ready, 1)
            over = pool.value_load(tiles_over[0:1, 0:1], min_val=0, max_val=OV)
            with pool.If(over > 0):
                with pool.Fori(0, OV) as k:
                    pool.wait_ge(o_fin, k + 1)
                    col = pool.value_load(over_column[0:1, bass.ds(k, 1)], min_val=0, max_val=EX * JT)
                    pool.tensor_copy(o_idx[:, :], lists[:, col, :]).then_inc(o_copied, 1)
                    pool.memset(o_x[:, :], 0.0).then_inc(o_copied, 1)
                    pool.memset(o_acc[:, :], 0.0).then_inc(o_copied, 1)
                    pool.wait_ge(o_copied, k * 3 + 3)
                    apart(pool)
                    for dst, src, s_ in ((o_x, xn_rows, o_xin), (o_acc, out_rows, o_ain)):
                        pool.indirect_dma_start(dst[:, :], None, src,
                                                bass.IndirectOffsetOnAxis(ap=o_idx[:, 0:1], axis=0),
                                                bounds_check=last_token, oob_is_err=False).then_inc(s_, 16)
                    pool.wait_ge(o_fin, k + 2)
                    apart(pool)
                    pool.indirect_dma_start(out_rows, bass.IndirectOffsetOnAxis(ap=o_idx[:, 0:1], axis=0),
                                            o_r[:, :], None, bounds_check=last_token,
                                            oob_is_err=False).then_inc(o_sto, 16)
                    pool.wait_ge(o_sto, k * 16 + 16)

        @block.scalar
        def _(act):
            act.wait_ge(small_loaded, 48)
            act.activation(etd[:, :], td[:, :], ACT.Exp).then_inc(decay_exp, 1)
            act.wait_ge(decay_exp, 1)
            act.activation(dd[:, :], etd[:, :], ACT.Exp, scale=-1.0).then_inc(decay_exp, 1)
            act.wait_ge(ln1, 1)
            act.activation(lnv[:, :], ve[:, :], ACT.Ln).then_inc(ln1_act, 1)
            act.wait_ge(ln1_act, 1)
            act.activation(r0[:, :], lnv[:, :], ACT.Exp, scale=-0.5).then_inc(ln1_act, 1)
            act.wait_ge(ln1, 1 + LN1_STEPS + 1)

            def high_part(dst, src, n):
                act.wait_ge(*n)
                return act.activation(dst, src, ACT.Copy)

            def exponentials(s, c):
                un = s * NC + c
                act.wait_ge(k_turned, un + 2)
                act.wait_ge(b_scanned, un + 1)
                act.activation(f1[:, c % 2, :], bank[c % 2][:, :], ACT.Exp, bias=ub1[:, c:c + 1])
                act.wait_ge(y_made, un + 1)
                act.activation(f2[:, c, :], bank[c % 2][:, :], ACT.Exp, bias=ub2[:, c:c + 1]).then_inc(f2_made, 1)
                act.wait_ge(v_turned, un + 1)
                act.wait_ge(g2_made, un + 1)
                act.activation(vs[:, c % 2, :], bank[2 + c % 2][:, :], ACT.Copy).then_inc(vs_made, 1)

            def inverse(s, c):
                un = s * NC + c
                fv = f2[:, c, :].rearrange("p (b t) -> p b t", t=T)[:, :, 1:T]
                act.wait_ge(den_made, un + 3)
                act.activation(fv, fv, ACT.Ln).then_inc(ln_made, 1)
                act.wait_ge(ln_made, un + 1)
                act.activation(fv, fv, ACT.Exp, scale=-1.0).then_inc(rden_made, 1)

            with act.Fori(0, NG) as s:
                act.wait_ge(k_turned, s * NC + 1)
                for j in range(GT):
                    t = s * GT + j
                    act.activation(K[:, j, :], X[:, t, :], ACT.Identity, bias=nm1[:, bass.ds(t, 1)],
                                   scale=rs1[:, bass.ds(t, 1)]).then_inc(k_ready, 1)
                exponentials(s, 0)
                for c in range(1, NC):
                    exponentials(s, c)
                    inverse(s, c - 1)
                for i in range(3):
                    if i == 0:
                        for m in range(3):
                            act.wait_ge(raw_loaded[m], 16)
                    act.activation(wh[0].rearrange("p m k n -> p (m k) n")[:, s * 3 + i, :],
                                   raw.rearrange("p m k n -> p (m k) n")[:, s * 3 + i, :],
                                   ACT.Copy).then_inc(wh_made, 1)
                inverse(s, NC - 1)
                for j in range(GT):
                    t = s * GT + j
                    act.wait_ge(x1_made, t + 3)
                    act.dma_start(out_rows[bass.ds(t * P, P), :], X[:, t, :]).then_inc(x1_stored, 16)
                act.wait_ge(ln2, s * (LN1_STEPS + 1) + 1)
                act.activation(lnv2[:, :], ve2[:, :], ACT.Ln).then_inc(ln2_act, 1)
                act.wait_ge(ln2_act, s * 2 + 1)
                act.activation(q0[:, :], lnv2[:, :], ACT.Exp, scale=-0.5).then_inc(ln2_act, 1)
                for j in range(GT):
                    t = s * GT + j
                    act.wait_ge(xn_made, t + 1)
                    act.dma_start(xn_rows[bass.ds(t * P, P), :], XN[:, j, :]).then_inc(xn_stored[j], 16)
                    act.wait_ge(xn_turned, t + 1)
                    act.wait_ge(gated, t + 1)
                    act.activation(XNT[:, j % 2, :, :], bank[6].rearrange("p (k n) -> p k n", n=P),
                                   ACT.Copy).then_inc(xnt_made, 1)
                act.wait_ge(delta_made, s + 1)
                act.activation(e2[:, :], dlt[:, :], ACT.Exp).then_inc(e2_made, 1)
                for j in range(GT):
                    act.wait_ge(xn_stored[j], s * 16 + 16)
                act.sem_inc(xn_free, 1)
            act.wait_ge(e2_made, NG)
            act.sem_inc(phase_a_done, 1)

            act.wait_ge(phase_a_done, 3)
            act.wait_ge(b_cleared, 2)

            def x_high(p, i):
                r, j, tt = i // CT, i % CT, p * 2 * CT + i
                act.wait_ge(xg_turned, tt + 3)
                act.activation(xth[r][:, :, j * P:(j + 1) * P], bank[6 + i % 2].rearrange("p (k n) -> p k n", n=P),
                               ACT.Copy).then_inc(xh_made, 1)

            def w_high(p, r, n):
                e, m = p * 2 + r, n // NK
                if n == 0:
                    act.wait_ge(out_done, e * CT + 1)
                if n % NK == 0:
                    act.wait_ge(raw_loaded[m], (e + 2) * 16)
                act.activation(wh[1 - r][:, m, n % NK, :], raw[:, m, n % NK, :], ACT.Copy).then_inc(wh_made, 1)

            def h_high(p, r, l):
                hb = (p * 2 + r) * 2 * NK + l
                act.wait_ge(hm_made, hb + 3)
                act.activation(hth[:, l % NK, (l // NK) * HW:(l // NK + 1) * HW], hm[:, l % 2, :],
                               ACT.Copy).then_inc(hh_made, 1)

            def silu(p, r, l):
                hb = (p * 2 + r) * 2 * NK + l
                act.wait_ge(h0_done, hb + 1)
                act.wait_ge(hm_made, hb + 1)
                act.activation(sl[:, l % 2, :], bank[l % 2][:, 0:HW], ACT.Silu).then_inc(silu_made, 1)

            def expert(p, r, last):
                nxt = [(p, CT + j) if r == 0 else (p + 1, j) for j in range(CT)]
                for l in range(2 * NK):
                    if l > 0:
                        h_high(p, r, l - 1)
                    silu(p, r, l)
                    if 2 <= l < 2 + CT and not last:
                        x_high(*nxt[l - 2])
                    if not last:
                        w_high(p, r, l)
                h_high(p, r, 2 * NK - 1)
                if not last:
                    for n in range(2 * NK, 3 * NK):
                        w_high(p, r, n)

            for j in range(CT):
                x_high(0, j)
            with act.Fori(0, EX // 2 - 1) as p:
                expert(p, 0, False)
                expert(p, 1, False)
            expert(EX // 2 - 1, 0, False)
            expert(EX // 2 - 1, 1, True)

            act.wait_ge(over_ready, 1)
            over = act.value_load(tiles_over[0:1, 0:1], min_val=0, max_val=OV)
            with act.If(over > 0):
                with act.Fori(0, OV) as k:
                    act.wait_ge(o_xturn, k + 1)
                    act.activation(o_xt[:, :, :], bank[6].rearrange("p (k n) -> p k n", n=P), ACT.Copy).then_inc(o_xtm, 1)
                    act.wait_ge(o_h01, k + 1)
                    act.activation(o_s[:, :], bank[0][:, :], ACT.Silu).then_inc(o_sm, 1)
                    act.wait_ge(o_hturn, k + 1)
                    act.activation(o_ht[:, :, :], bank[7].rearrange("p (k n) -> p k n", n=P), ACT.Copy).then_inc(o_htm, 1)

        @block.vector
        def _(dve):
            def inv_sqrt(v, start, a, b, c, r, sem_, base, n):
                steps = (lambda: dve.tensor_tensor(a, start, start, ALU.mult),
                         lambda: dve.tensor_tensor(b, a, v, ALU.mult),
                         lambda: dve.tensor_scalar(c, b, -0.5, 1.5, ALU.mult, ALU.add),
                         lambda: dve.tensor_tensor(r, c, start, ALU.mult))
                for i in range(len(steps)):
                    steps[i]().then_inc(sem_, 1)
                    dve.wait_ge(sem_, base + i + 1)

            dve.memset(decay_row[:, :, :], 1.0).then_inc(dve_prologue, 1)
            dve.wait_ge(small_loaded, 48)
            dve.tensor_scalar(ub1[:, :], tf[:, :], 0.0, -1.0, ALU.max, ALU.mult)
            dve.tensor_scalar(ub2[:, :], tf[:, :], 0.0, None, ALU.min)
            for g in range(NG):
                dve.wait_ge(x_loaded[g], 16)
                for t in range(g * GT, (g + 1) * GT):
                    dve.bn_stats(stat1[:, t, :], X[:, t, :]).then_inc(dve_prologue, 1)
            for t in range(NT):
                dve.wait_ge(dve_prologue, 2 + t)
                last = dve.bn_aggr(mv1[:, t, :], stat1[:, t, :])
            last.then_inc(dve_prologue, 1)
            dve.wait_ge(dve_prologue, 2 + NT)
            dve.tensor_scalar(ve[:, :], mv1[:, :, 1], EPS, None, ALU.add).then_inc(ln1, 1)
            dve.wait_ge(decay_exp, 2)
            for c in range(NC):
                last = dve.tensor_scalar(decay_row[:, c, :], decay_row[:, c, :], dd[:, c:c + 1], None, ALU.mult)
            last.then_inc(dve_prologue, 1)
            dve.wait_ge(dve_prologue, 3 + NT)
            dve.memset(decay_row[:, :, T:T + 1], 0.0).then_inc(dve_prologue, 1)
            dve.wait_ge(dve_prologue, 4 + NT)
            dve.wait_ge(ln1_act, 2)
            dve.wait_ge(ln1, 1)
            inv_sqrt(ve[:, :], r0[:, :], na[:, :], nb[:, :], ncf[:, :], rs1[:, :], ln1, 1, NT)
            dve.scalar_tensor_tensor(nm1[:, :], mv1[:, :, 0], -1.0, rs1[:, :], ALU.mult, ALU.mult).then_inc(ln1, 1)
            dve.sem_inc(rows_made, 1)

            def finish_y(s, c):
                un = s * NC + c
                yv, nv, rv = (z.rearrange("p (b t) -> p b t", t=T)[:, :, 1:T]
                              for z in (Y[:, c, :], g2[:, c % 2, :], f2[:, c, :]))
                dve.wait_ge(num_made, un + 1)
                dve.wait_ge(rden_made, un + 1)
                if c == 0:
                    dve.wait_ge(y_turned, s * GT + 1)
                dve.tensor_tensor(yv, nv, rv, ALU.mult).then_inc(y_made, 1)

            def unit(s, c):
                un, q = s * NC + c, c % 2
                dve.wait_ge(f2_made, un + 3)
                dve.wait_ge(vs_made, un + 3)
                dve.tensor_tensor(g1[:, q, :], f1[:, q, :], vs[:, q, :], ALU.mult).then_inc(g1_made, 1)
                dve.wait_ge(den_made, un + 1)
                dve.tensor_tensor_scan(st_b[:, q, 1:GW], decay_row[:, c, 0:GW - 1], f1[:, q, 0:GW - 1], 0.0,
                                       ALU.mult, ALU.add).then_inc(b_scanned, 1)
                dve.wait_ge(g1_made, un + 1)
                dve.tensor_tensor_scan(st_a[:, q, 1:GW], decay_row[:, c, 0:GW - 1], g1[:, q, 0:GW - 1], 0.0,
                                       ALU.mult, ALU.add).then_inc(a_scanned, 1)
                if c > 0:
                    finish_y(s, c - 1)
                gv, av = (z.rearrange("p (b t) -> p b t", t=T)[:, :, 1:T] for z in (g2[:, q, :], st_a[:, q, :]))
                dve.wait_ge(g2_made, un + 3)
                dve.wait_ge(a_scanned, un + 1)
                dve.tensor_tensor(gv, gv, av, ALU.add).then_inc(num_made, 1)

            def w_low(h, l, r):
                return dve.tensor_tensor(l, r, h.bitcast(F32), ALU.subtract)

            def routing(s):
                n = [0]

                def step(ins):
                    n[0] += 1
                    ins.then_inc(route, 1)
                    dve.wait_ge(route, s * ROUTE_STEPS + n[0])

                dve.wait_ge(gated, s * GT + GT + 2)
                dve.wait_ge(rec_stored, (s + 1) * 16 * 2 * GT)
                step(dve.tensor_copy(lg[:, :, :], logits))
                apart(dve)
                for j in range(GT):
                    ins = dve.max(m8[:, j, :], lg[:, j, :])
                step(ins)
                apart(dve)
                for j in range(GT):
                    ins = dve.max_index(i8[:, j, :], m8[:, j, :], lg[:, j, :])
                step(ins)
                dve.tensor_tensor(dlt[:, :], m8[:, :, 1], m8[:, :, 0], ALU.subtract).then_inc(delta_made, 1)
                step(dve.tensor_copy(idxf[:, :, :], i8[:, :, 0:2]))
                step(dve.tensor_tensor(oh[:, :, :, :],
                                       iota8[:, None, None, :].to_broadcast([P, GT, 2, EX]),
                                       idxf[:, :, :, None].to_broadcast([P, GT, 2, EX]), ALU.is_equal))
                step(dve.tensor_tensor(msk[:, :, :], oh[:, :, 0, :], oh[:, :, 1, :], ALU.add))
                for j in range(GT):
                    ins = dve.tensor_tensor(cum[:, j + 1, :], cum[:, j, :], msk[:, j, :], ALU.add)
                    if j < GT - 1:
                        step(ins)
                ins.then_inc(mask_made, 1)
                step(dve.tensor_scalar(ebs[:, :, :], i8[:, :, 0:2].bitcast(I32), NTOK.bit_length() - 1, None,
                                       ALU.logical_shift_left))
                dve.wait_ge(e2_made, s + 1)
                step(dve.tensor_scalar(e2p[:, :], e2[:, :], 1.0, None, ALU.add))
                step(dve.reciprocal(p1[:, :], e2p[:, :]))
                recf = rec.bitcast(F32)
                step(dve.tensor_copy(recf[:, :, 0, 1], p1[:, :]))
                step(dve.tensor_tensor(recf[:, :, 1, 1], p1[:, :], e2[:, :], ALU.mult))
                for q in range(2):
                    ins = dve.tensor_copy(rec[:, :, q, 0], tok[:, bass.ds(s * GT, GT)])
                step(ins)
                dve.wait_ge(ranked, s + 1)
                step(dve.tensor_tensor(ohr[:, :, :, :], oh[:, :, :, :],
                                       ranks[:, :, None, :].to_broadcast([P, GT, 2, EX]), ALU.mult))
                dve.tensor_copy(cum[:, 0, :], cum[:, GT, :]).then_inc(ranks_read, 1)
                step(dve.tensor_reduce(rk[:, :, :], ohr[:, :, :, :], AX.X, ALU.add))
                step(dve.tensor_copy(rki[:, :, :], rk[:, :, :]))
                step(dve.tensor_scalar(lo7[:, :, :], rki[:, :, :], P - 1, JT.bit_length() - 1,
                                       ALU.bitwise_and, ALU.logical_shift_left))
                step(dve.tensor_scalar(hi4[:, :, :], rki[:, :, :], P.bit_length() - 1, None,
                                       ALU.logical_shift_right))
                step(dve.tensor_tensor(lh[:, :, :], lo7[:, :, :], hi4[:, :, :], ALU.bitwise_or))
                dve.tensor_tensor(row[:, :, :], lh[:, :, :], ebs[:, :, :], ALU.bitwise_or).then_inc(rows_made, 1)
                assert n[0] == ROUTE_STEPS, n[0]

            dve.wait_ge(const_made, 2)
            with dve.Fori(0, NG) as s:
                for c in range(NC):
                    unit(s, c)
                for i in range(3):
                    dve.wait_ge(wh_made, s * 3 + i + 1)
                    flat = [z.rearrange("p m k n -> p (m k) n")[:, s * 3 + i, :] for z in (wh[0], wl[0], raw)]
                    w_low(*flat).then_inc(wl_made, 1)
                finish_y(s, NC - 1)
                for j in range(GT):
                    t = s * GT + j
                    dve.wait_ge(y_turned, t + 2)
                    dve.tensor_tensor(X[:, t, :], X[:, t, :], bank[4 + j % 2][:, :], ALU.add).then_inc(x1_made, 1)
                    dve.wait_ge(x1_made, t + 3)
                    apart(dve)
                    dve.bn_stats(stat2[:, j, :], X[:, t, :]).then_inc(stat2_made, 1)
                for j in range(GT):
                    dve.wait_ge(stat2_made, s * GT + j + 1)
                    apart(dve)
                    ins = dve.bn_aggr(mv2[:, j, :], stat2[:, j, :])
                ins.then_inc(mv2_made, 1)
                dve.wait_ge(mv2_made, s + 1)
                dve.tensor_scalar(ve2[:, :], mv2[:, :, 1], EPS, None, ALU.add).then_inc(ln2, 1)
                dve.wait_ge(ln2_act, s * 2 + 2)
                dve.wait_ge(ln2, s * (LN1_STEPS + 1) + 1)
                inv_sqrt(ve2[:, :], q0[:, :], qa[:, :], qb[:, :], qc[:, :], rs2[:, :], ln2,
                         s * (LN1_STEPS + 1) + 1, GT)
                dve.wait_ge(xn_free, s + 1)
                for j in range(GT):
                    dve.tensor_scalar(XN[:, j, :], X[:, s * GT + j, :], mv2[:, j, 0:1], rs2[:, j:j + 1],
                                      ALU.subtract, ALU.mult).then_inc(xn_made, 1)
                routing(s)
            dve.wait_ge(rows_made, NG + 1)
            dve.wait_ge(totals_made, 1)
            dve.tensor_copy(totals[:, :], bank[7][:, 128:128 + EX]).then_inc(over_made, 1)
            dve.wait_ge(over_made, 1)
            dve.sem_inc(phase_a_done, 1)

            dve.wait_ge(phase_a_done, 3)
            dve.wait_ge(b_cleared, 2)

            def x_low(p, i):
                r, j, tt = i // CT, i % CT, p * 2 * CT + i
                dve.wait_ge(xh_made, tt + 1)
                dve.tensor_tensor(xtl[r][:, :, j * P:(j + 1) * P], bank[6 + i % 2].rearrange("p (k n) -> p k n", n=P),
                                  xth[r][:, :, j * P:(j + 1) * P].bitcast(F32), ALU.subtract).then_inc(xl_made, 1)

            def wl_chunk(p, r, n):
                e, m = p * 2 + r, n // NK
                dve.wait_ge(wh_made, (e + 1) * 3 * NK + n + 1)
                w_low(wh[1 - r][:, m, n % NK, :], wl[1 - r][:, m, n % NK, :], raw[:, m, n % NK, :]).then_inc(wl_made, 1)

            def h_low(p, r, l):
                hb = (p * 2 + r) * 2 * NK + l
                w = slice((l // NK) * HW, (l // NK + 1) * HW)
                dve.wait_ge(hh_made, hb + 1)
                dve.tensor_tensor(htl[:, l % NK, w], hm[:, l % 2, :], hth[:, l % NK, w].bitcast(F32),
                                  ALU.subtract).then_inc(hl_made, 1)

            def gated_product(p, r, l):
                hb = (p * 2 + r) * 2 * NK + l
                dve.wait_ge(silu_made, hb + 3)
                dve.wait_ge(h1_done, hb + 1)
                dve.tensor_tensor(hm[:, l % 2, :], bank[2 + l % 2][:, 0:HW], sl[:, l % 2, :],
                                  ALU.mult).then_inc(hm_made, 1)

            listf = lists.bitcast(F32)

            def finish(p, r, j):
                e = p * 2 + r
                tt = e * CT + j
                dve.wait_ge(out_done, tt + 2)
                dve.wait_ge(acc_loaded[j], (e + 1) * 16)
                dve.scalar_tensor_tensor(acc[:, j, :], bank[4 + (r * CT + j) % 2][:, :],
                                         listf[:, e * JT + j, 1:2], acc[:, j, :],
                                         ALU.mult, ALU.add).then_inc(fin_made, 1)

            def expert(p, r, last):
                nxt = [(p, CT + j) if r == 0 else (p + 1, j) for j in range(CT)]
                for l in range(2 * NK):
                    if l > 0:
                        h_low(p, r, l - 1)
                    if 2 <= l < 2 + CT and not last:
                        x_low(*nxt[l - 2])
                    if not last:
                        wl_chunk(p, r, l)
                    gated_product(p, r, l)
                h_low(p, r, 2 * NK - 1)
                for j in range(CT):
                    if not last and j < NK:
                        wl_chunk(p, r, 2 * NK + j)
                    finish(p, r, j)

            for j in range(CT):
                x_low(0, j)
            dve.wait_ge(lists_loaded, 16)
            with dve.Fori(0, EX // 2 - 1) as p:
                expert(p, 0, False)
                expert(p, 1, False)
            expert(EX // 2 - 1, 0, False)
            expert(EX // 2 - 1, 1, True)

            n = [1]

            def step(ins):
                n[0] += 1
                ins.then_inc(over_made, 1)
                dve.wait_ge(over_made, n[0])

            step(dve.tensor_scalar(cnt_f[:, :], totals[:, :], float(P - 1), None, ALU.add))
            step(dve.tensor_copy(cnt_b[:, :], cnt_f[:, :]))
            step(dve.tensor_scalar(cnt_t[:, :], cnt_b[:, :], P.bit_length() - 1, None, ALU.logical_shift_right))
            step(dve.tensor_copy(cnt_f[:, :], cnt_t[:, :]))
            step(dve.tensor_scalar(extra[:, :], cnt_f[:, :], -float(CT), 0.0, ALU.add, ALU.max))
            step(dve.tensor_tensor_scan(extra_sum[:, :], ones8[:, :], extra[:, :], 0.0, ALU.mult, ALU.add))
            step(dve.tensor_copy(tiles_over[:, :], extra_sum[:, EX - 1:EX]))
            step(dve.tensor_tensor(past[:, :, :], over_iota[:, :, None].to_broadcast([P, OV, EX]),
                                   extra_sum[:, None, :].to_broadcast([P, OV, EX]), ALU.is_ge))
            step(dve.tensor_tensor(past_n[:, :, :], past[:, :, :],
                                   extra[:, None, :].to_broadcast([P, OV, EX]), ALU.mult))
            step(dve.tensor_reduce(past_experts[:, :], past[:, :, :], AX.X, ALU.add))
            step(dve.tensor_reduce(past_tiles[:, :], past_n[:, :, :], AX.X, ALU.add))
            step(dve.tensor_tensor(over_j[:, :], over_iota[:, :], past_tiles[:, :], ALU.subtract))
            step(dve.scalar_tensor_tensor(over_c[:, :], past_experts[:, :], float(JT), over_j[:, :],
                                          ALU.mult, ALU.add))
            step(dve.tensor_scalar(over_d[:, :], over_c[:, :], float(CT), float(EX * JT), ALU.add, ALU.min))
            step(dve.tensor_copy(over_column[:, :], over_d[:, :]))
            step(dve.tensor_scalar(over_j[:, :], past_experts[:, :], float(EX - 1), None, ALU.min))
            step(dve.tensor_copy(over_expert[:, :], over_j[:, :]))
            dve.sem_inc(over_ready, 1)
            over = dve.value_load(tiles_over[0:1, 0:1], min_val=0, max_val=OV)
            with dve.If(over > 0):
                with dve.Fori(0, OV) as k:
                    dve.wait_ge(o_sm, k + 1)
                    dve.wait_ge(o_h01, k + 1)
                    dve.wait_ge(o_copied, k * 3 + 3)
                    dve.tensor_tensor(o_h[:, :], bank[2][:, :], o_s[:, :], ALU.mult).then_inc(o_hm, 1)
                    dve.wait_ge(o_out, k + 1)
                    dve.wait_ge(o_ain, k * 16 + 16)
                    dve.scalar_tensor_tensor(o_r[:, :], bank[4][:, :], o_idx.bitcast(F32)[:, 1:2], o_acc[:, :],
                                             ALU.mult, ALU.add).then_inc(o_fin, 1)

        @block.tensor
        def _(pe):
            pe.wait_ge(ident_made, 2)
            pe.wait_ge(const_made, 2)
            pe.wait_ge(small_loaded, 48)
            with pe.Fori(0, NG) as s:
                for c in range(NC):
                    un = s * NC + c
                    ch = slice(c * P, (c + 1) * P)
                    if c == 0:
                        pe.wait_ge(k_ready, s * GT + GT)
                    pe.wait_ge(f2_made, un + 1)
                    for j in range(GT):
                        ins = pe.transpose(bank[c % 2][:, j * P:(j + 1) * P], K[:, j, ch], ident[:, :])
                    ins.then_inc(k_turned, 1)
                    if c == 0:
                        pe.wait_ge(v_loaded, s * 16 + 16)
                    pe.wait_ge(vs_made, un + 1)
                    for j in range(GT):
                        ins = pe.transpose(bank[2 + c % 2][:, j * P:(j + 1) * P], V[:, j, ch], ident[:, :])
                    ins.then_inc(v_turned, 1)
                pe.wait_ge(y_made, s * NC + NC + 4)
                pe.wait_ge(g2_made, s * NC + NC + 2)
                for j in range(GT):
                    pe.wait_ge(x1_made, s * GT + j + 1)
                    for c in range(NC):
                        ins = pe.transpose(bank[4 + j % 2][:, c * P:(c + 1) * P], Y[:, c, j * P:(j + 1) * P],
                                           ident[:, :])
                    ins.then_inc(y_turned, 1)

                def router(j):
                    t = s * GT + j
                    pe.wait_ge(xnt_made, t + 2)
                    if j == 0:
                        pe.wait_ge(ranks_read, s + 1)
                    for c in range(NC):
                        ins = pe.matmul(logits[:, j, :], XNT[:, j % 2, c, :], gk[:, c, :],
                                        start=(c == 0), stop=(c == NC - 1))
                    ins.then_inc(gated, 1)

                for j in range(GT):
                    t = s * GT + j
                    pe.wait_ge(xn_made, t + 1)
                    pe.wait_ge(xnt_made, t + 1)
                    for c in range(NC):
                        ins = pe.transpose(bank[6][:, c * P:(c + 1) * P], XN[:, j, c * P:(c + 1) * P], ident[:, :])
                    ins.then_inc(xn_turned, 1)
                    router(j)
                pe.wait_ge(mask_made, s + 1)
                pe.matmul(ranks, before[:, :], msk[:, :, :], start=True, stop=False)
                pe.matmul(ranks, ones[:, :], cum[:, 0:GT, :], start=False, stop=True).then_inc(ranked, 1)
            pe.wait_ge(ranks_read, NG + 1)
            pe.matmul(bank[7][:, 128:128 + EX], ones[:, :], cum[:, 0, :], start=True, stop=True).then_inc(totals_made, 1)
            pe.wait_ge(totals_made, 1)
            pe.sem_inc(phase_a_done, 1)

            pe.wait_ge(over_made, 1)
            pe.wait_ge(b_cleared, 2)

            def turn_x(p, i):
                tt = p * 2 * CT + i
                pe.wait_ge(xg_loaded[i % 2], (p * CT + i // 2 + 1) * 16)
                pe.wait_ge(xl_made, tt + 1)
                for c in range(NK):
                    ins = pe.transpose(bank[6 + i % 2][:, c * P:(c + 1) * P], xg[:, i % 2, c * P:(c + 1) * P],
                                       ident[:, :])
                ins.then_inc(xg_turned, 1)

            def split_product(dst, parts):
                terms = [t for lh_, ll_, rh_, rl_ in parts for t in ((lh_, rh_), (lh_, rl_), (ll_, rh_))]
                for i, (a, b_) in enumerate(terms):
                    ins = pe.matmul(dst, a, b_, start=(i == 0), stop=(i == len(terms) - 1))
                return ins

            def hidden(p, r, l):
                e, half, mb = p * 2 + r, l // NK, l % NK
                hb = e * 2 * NK + l
                w, mc = slice(half * HW, (half + 1) * HW), slice(mb * P, (mb + 1) * P)
                if l == 0:
                    pe.wait_ge(wl_made, e * 3 * NK + NK)
                    pe.wait_ge(xl_made, e * CT + (HW + P - 1) // P + 2)
                if l == NK:
                    pe.wait_ge(xl_made, e * CT + CT + 2)
                for m, free, done in ((0, silu_made, h0_done), (1, hm_made, h1_done)):
                    if l == 0 and m == 1:
                        pe.wait_ge(wl_made, e * 3 * NK + 2 * NK)
                    pe.wait_ge(free, hb + 1)
                    split_product(bank[2 * m + l % 2][:, 0:HW],
                                  [(wh[r][:, m, k, mc], wl[r][:, m, k, mc], xth[r][:, k, w], xtl[r][:, k, w])
                                   for k in range(NK)]).then_inc(done, 1)

            def output(p, r, j):
                e = p * 2 + r
                tw = slice(j * P, (j + 1) * P)
                if j == 0:
                    pe.wait_ge(wl_made, (e + 1) * 3 * NK)
                pe.wait_ge(hl_made, e * 2 * NK + (NK if (j + 1) * P <= HW else 2 * NK))
                pe.wait_ge(fin_made, e * CT + j + 1)
                split_product(bank[4 + (r * CT + j) % 2][:, :],
                              [(hth[:, k, tw], htl[:, k, tw], wh[r][:, 2, k, :], wl[r][:, 2, k, :])
                               for k in range(NK)]).then_inc(out_done, 1)

            def expert(p, r, last):
                nxt = [(p, CT + j) if r == 0 else (p + 1, j) for j in range(CT)]
                for l in range(2 * NK):
                    hidden(p, r, l)
                    if 1 <= l < 1 + CT and not last:
                        turn_x(*nxt[l - 1])
                for j in range(CT):
                    output(p, r, j)

            for j in range(CT):
                turn_x(0, j)
            with pe.Fori(0, EX // 2 - 1) as p:
                expert(p, 0, False)
                expert(p, 1, False)
            expert(EX // 2 - 1, 0, False)
            expert(EX // 2 - 1, 1, True)

            pe.wait_ge(fin_made, EX * CT + 2)
            pe.wait_ge(over_ready, 1)
            over = pe.value_load(tiles_over[0:1, 0:1], min_val=0, max_val=OV)
            with pe.If(over > 0):
                with pe.Fori(0, OV) as k:
                    pe.wait_ge(o_xin, k * 16 + 16)
                    for c in range(NK):
                        ins = pe.transpose(bank[6][:, c * P:(c + 1) * P], o_x[:, c * P:(c + 1) * P], ident[:, :])
                    ins.then_inc(o_xturn, 1)
                    pe.wait_ge(o_xtm, k + 1)
                    pe.wait_ge(o_w, k * 48 + 48)
                    for m in range(2):
                        for c in range(NK):
                            ins = pe.matmul(bank[2 * m][:, :], o_xt[:, c, :], raw[:, m, c, :],
                                            start=(c == 0), stop=(c == NK - 1))
                    ins.then_inc(o_h01, 1)
                    pe.wait_ge(o_hm, k + 1)
                    for c in range(NK):
                        ins = pe.transpose(bank[7][:, c * P:(c + 1) * P], o_h[:, c * P:(c + 1) * P], ident[:, :])
                    ins.then_inc(o_hturn, 1)
                    pe.wait_ge(o_htm, k + 1)
                    for c in range(NK):
                        ins = pe.matmul(bank[4][:, :], o_ht[:, c, :], raw[:, 2, c, :],
                                        start=(c == 0), stop=(c == NK - 1))
                    ins.then_inc(o_out, 1)


def kernel(x, ctx_2048, L0_xattn_time_decay, L0_xattn_time_first, L0_ffn_gate_kernel,
           L0_ffn_wi_0, L0_ffn_wi_1, L0_ffn_wo):
    import numpy as np
    import concourse.bacc as bacc
    from concourse.bass_utils import run_bass_kernel_spmd

    nc = bacc.Bacc("TRN2", target_bir_lowering=False, num_devices=1)
    arrays = {
        "in_x": np.ascontiguousarray(x),
        "in_ctx": np.ascontiguousarray(ctx_2048),
        "in_decay": np.ascontiguousarray(np.asarray(L0_xattn_time_decay).reshape(NC, P).T),
        "in_first": np.ascontiguousarray(np.asarray(L0_xattn_time_first).reshape(NC, P).T),
        "in_gate": np.ascontiguousarray(np.asarray(L0_ffn_gate_kernel).reshape(NC, P, EX).transpose(1, 0, 2)),
        "in_wi0": np.ascontiguousarray(L0_ffn_wi_0),
        "in_wi1": np.ascontiguousarray(L0_ffn_wi_1),
        "in_wo": np.ascontiguousarray(L0_ffn_wo),
    }
    args = [nc.dram_tensor(n, a.shape, mybir.dt.from_np(a.dtype), kind="ExternalInput").ap()
            for n, a in arrays.items()]
    out = nc.dram_tensor("out_x", (B, T, C), F32, kind="ExternalOutput").ap()
    build(nc, *args, out)
    r = run_bass_kernel_spmd(nc, [arrays], core_ids=[0])
    return r.results[0]["out_x"]
```

```python
from contextlib import ExitStack

import concourse.bass as bass
from concourse import mybir

P = 128
B, T, C = 8, 256, 512
NTOK = B * T
NT = NTOK // P
NC = C // P
GT = 4
NG = NT // GT
GW = GT * P
EX, M = 8, 512
NK = C // P
EPS = 1e-5
EXP_LN_SET = 6
CT = 5
CAP = CT * P
FT = CT // 2
PARTS = (slice(0, FT * P), slice(FT * P, CAP))
JT = NT
OOB = NTOK
OV = max(n * min(JT - CT, JT) if 2 * n <= 4 else (2 * NTOK + n * (P - 1)) // P - CT * n
         for n in range(1, EX + 1) if n <= 2 or (2 * NTOK + n * (P - 1)) // P - CT * n > 0)

F32, F32R = mybir.dt.float32, mybir.dt.float32r
BF16, I32, U32 = mybir.dt.bfloat16, mybir.dt.int32, mybir.dt.uint32
ALU, ACT, AX = mybir.AluOpType, mybir.ActivationFunctionType, mybir.AxisListType


def build(nc, x, ctx, decay, first, gate, wi0, wi1, wo, out):
    weights = [w.rearrange("e (k p) m -> e p k m", p=P) for w in (wi0, wi1, wo)]
    x_in = x.rearrange("b (h p) c -> p (b h) c", p=P)
    v_in = ctx.rearrange("b (h p) c -> p (b h) c", p=P)
    out_rows = out.rearrange("b t c -> (b t) c")
    xn_rows = nc.dram_tensor("xn_rows", [NTOK, C], F32, kind="Internal").ap()
    table = nc.dram_tensor("table", [EX * NTOK, 2], I32, kind="Internal").ap()

    with ExitStack() as keep:
        def sb(name, shape, dt=F32, stack=keep):
            return stack.enter_context(nc.sbuf_tensor(name, shape, dt))

        def sem(name):
            return keep.enter_context(nc.semaphore(name))

        raw = sb("raw", [P, 3, NK, M])
        wh = [sb("wh0", [P, 3, NK, M], F32R), None]
        wl = [sb("wl0", [P, 3, NK, M], F32R), None]
        ident = sb("ident", [P, P])
        before = sb("before", [P, P], BF16)
        ones = sb("ones", [P, P], BF16)
        lists = sb("lists", [P, EX * JT + 1, 2], I32)
        totals = sb("totals", [P, EX])
        xg = sb("xg", [P, 2, C])
        acc = sb("acc", [P, CT, C])
        idx = sb("idx", [P, 2, CT], I32)
        tiles_over = sb("tiles_over", [P, 1], I32)
        over_expert = sb("over_expert", [P, OV], I32)
        over_column = sb("over_column", [P, OV], I32)
        over_iota = sb("over_iota", [P, OV])
        ones8 = sb("ones8", [P, EX])
        cnt_b = sb("cnt_b", [P, EX], I32); cnt_t = sb("cnt_t", [P, EX], I32)
        cnt_f = sb("cnt_f", [P, EX]); extra = sb("extra", [P, EX]); extra_sum = sb("extra_sum", [P, EX])
        past = sb("past", [P, OV, EX]); past_n = sb("past_n", [P, OV, EX])
        past_experts = sb("past_experts", [P, OV]); past_tiles = sb("past_tiles", [P, OV])
        over_j = sb("over_j", [P, OV]); over_c = sb("over_c", [P, OV]); over_d = sb("over_d", [P, OV])

        phase_a = ExitStack()
        def sa(name, shape, dt=F32):
            return sb(name, shape, dt, phase_a)
        X = sa("X", [P, NT, C])
        K = sa("K", [P, GT, C])
        V = sa("V", [P, GT, C])
        decay_row = sa("decay_row", [P, NC, GW])
        f1 = sa("f1", [P, 2, GW])
        f2 = sa("f2", [P, 4, GW])
        vs = sa("vs", [P, 2, GW])
        g1 = sa("g1", [P, 2, GW])
        g2 = sa("g2", [P, 2, GW])
        st_a = sa("st_a", [P, 2, GW])
        st_b = sa("st_b", [P, 2, GW])
        Y = sa("Y", [P, NC, GW])
        XN = sa("XN", [P, GT, C])
        XNT = sa("XNT", [P, 2, NC, P])
        stat1 = sa("stat1", [P, NT, 6])
        mv1 = sa("mv1", [P, NT, 2])
        stat2 = sa("stat2", [P, GT, 6])
        mv2 = sa("mv2", [P, GT, 2])
        ve = sa("ve", [P, NT]); r0 = sa("r0", [P, NT]); na = sa("na", [P, NT]); nb = sa("nb", [P, NT])
        ncf = sa("ncf", [P, NT]); rs1 = sa("rs1", [P, NT]); nm1 = sa("nm1", [P, NT])
        ve2 = sa("ve2", [P, GT]); q0 = sa("q0", [P, GT]); qa = sa("qa", [P, GT]); qb = sa("qb", [P, GT])
        qc = sa("qc", [P, GT]); rs2 = sa("rs2", [P, GT]); nm2 = sa("nm2", [P, GT]); lnv = sa("lnv", [P, NT]); lnv2 = sa("lnv2", [P, GT])
        td = sa("td", [P, NC]); tf = sa("tf", [P, NC]); etd = sa("etd", [P, NC]); dd = sa("dd", [P, NC])
        ub1 = sa("ub1", [P, NC]); ub2 = sa("ub2", [P, NC])
        gk = sa("gk", [P, NC, EX])
        iota8 = sa("iota8", [P, EX])
        tok = sa("tok", [P, NT], I32)
        lg = sa("lg", [P, GT, EX]); m8 = sa("m8", [P, GT, 8]); i8 = sa("i8", [P, GT, 8], U32)
        idxf = sa("idxf", [P, GT, 2]); dlt = sa("dlt", [P, GT]); e2 = sa("e2", [P, GT])
        e2p = sa("e2p", [P, GT]); p1 = sa("p1", [P, GT])
        oh = sa("oh", [P, GT, 2, EX]); ohr = sa("ohr", [P, GT, 2, EX])
        msk = sa("msk", [P, GT, EX], BF16)
        cum = sa("cum", [P, GT + 1, EX], BF16)
        rk = sa("rk", [P, GT, 2]); rki = sa("rki", [P, GT, 2], I32); lo7 = sa("lo7", [P, GT, 2], I32)
        hi4 = sa("hi4", [P, GT, 2], I32); ebs = sa("ebs", [P, GT, 2], I32); lh = sa("lh", [P, GT, 2], I32)
        row = sa("row", [P, GT, 2], I32)
        rec = sa("rec", [P, GT, 2, 2], I32)
        blank = sa("blank", [P, P, 2], I32)
        phase_a.close()

        phase_b = ExitStack()
        def sbb(name, shape, dt=F32):
            return sb(name, shape, dt, phase_b)
        wh[1] = sbb("wh1", [P, 3, NK, M], F32R)
        wl[1] = sbb("wl1", [P, 3, NK, M], F32R)
        xth = [sbb(f"xth{i}", [P, NK, CAP], F32R) for i in range(2)]
        xtl = [sbb(f"xtl{i}", [P, NK, CAP], F32R) for i in range(2)]
        hth = sbb("hth", [P, NK, CAP], F32R)
        htl = sbb("htl", [P, NK, CAP], F32R)
        sl = sbb("sl", [P, 2, (CT - FT) * P])
        hm = sbb("hm", [P, 2, (CT - FT) * P])
        phase_b.close()

        phase_c = ExitStack()
        def sc(name, shape, dt=F32):
            return sb(name, shape, dt, phase_c)
        o_idx = sc("o_idx", [P, 2], I32)
        o_x = sc("o_x", [P, C]); o_acc = sc("o_acc", [P, C]); o_xt = sc("o_xt", [P, NK, P])
        o_s = sc("o_s", [P, M]); o_h = sc("o_h", [P, M]); o_ht = sc("o_ht", [P, NK, P]); o_r = sc("o_r", [P, C])
        phase_c.close()

        bank = [keep.enter_context(nc.psum_tensor(f"bank{i}", [P, 512], F32)) for i in range(8)]
        logits = bank[6][:, 0:GT * EX].rearrange("p (j e) -> p j e", e=EX)
        ranks = bank[6][:, 64:64 + GT * EX].rearrange("p (j e) -> p j e", e=EX)

        x_loaded = [sem(f"x_loaded{g}") for g in range(NG)]
        small_loaded = sem("small_loaded")
        v_loaded = sem("v_loaded")
        blank_made = sem("blank_made"); table_blank = sem("table_blank")
        const_made = sem("const_made"); ident_made = sem("ident_made")
        decay_exp = sem("decay_exp"); dve_prologue = sem("dve_prologue")
        ln1 = sem("ln1"); ln1_act = sem("ln1_act"); ln1_stat = sem("ln1_stat"); ln1_sum = sem("ln1_sum")
        k_ready = sem("k_ready")
        k_turned = sem("k_turned")
        v_turned = sem("v_turned")
        f2_made = sem("f2_made")
        vs_made = sem("vs_made")
        b_scanned = sem("b_scanned")
        g1_made = sem("g1_made")
        a_scanned = sem("a_scanned")
        den_made = sem("den_made")
        g2_made = sem("g2_made")
        first_made = sem("first_made")
        num_made = sem("num_made")
        y_made = sem("y_made")
        ln_made = sem("ln_made"); rden_made = sem("rden_made")
        y_turned = sem("y_turned")
        x1_made = sem("x1_made")
        x1_stored = sem("x1_stored")
        xn_stored = [sem(f"xn_stored{j}") for j in range(GT)]
        xn_free = sem("xn_free")
        ln2 = sem("ln2"); ln2_act = sem("ln2_act")
        stat2_made = sem("stat2_made"); mv2_made = sem("mv2_made")
        xn_made = sem("xn_made")
        xn_turned = sem("xn_turned")
        xnt_made = sem("xnt_made")
        gated = sem("gated")
        route = sem("route")
        mask_made = sem("mask_made"); delta_made = sem("delta_made"); e2_made = sem("e2_made")
        ranked = sem("ranked")
        ranks_read = sem("ranks_read")
        rows_made = sem("rows_made")
        rec_stored = sem("rec_stored")
        row_init = sem("row_init")
        totals_made = sem("totals_made")
        raw_loaded = [sem(f"raw_loaded{m}") for m in range(3)]
        wh_made = sem("wh_made"); wl_made = sem("wl_made")
        lists_loaded = sem("lists_loaded")
        phase_a_done = sem("phase_a_done")
        b_cleared = sem("b_cleared")
        idx_made = sem("idx_made")
        xg_loaded = [sem(f"xg_loaded{i}") for i in range(2)]
        xg_turned = sem("xg_turned")
        xh_made = sem("xh_made")
        xl_made = sem("xl_made")
        h0_done = sem("h0_done"); h1_done = sem("h1_done")
        silu_made = sem("silu_made")
        hm_made = sem("hm_made")
        hh_made = sem("hh_made"); hl_made = sem("hl_made")
        out_done = sem("out_done")
        fin_made = sem("fin_made")
        acc_loaded = [sem(f"acc_loaded{j}") for j in range(CT)]
        acc_stored = [sem(f"acc_stored{j}") for j in range(CT)]
        over_made = sem("over_made"); over_ready = sem("over_ready")
        o_w = sem("o_w"); o_copied = sem("o_copied"); o_xin = sem("o_xin"); o_ain = sem("o_ain")
        o_xturn = sem("o_xturn"); o_xtm = sem("o_xtm"); o_h01 = sem("o_h01"); o_sm = sem("o_sm")
        o_hm = sem("o_hm"); o_hturn = sem("o_hturn"); o_htm = sem("o_htm"); o_out = sem("o_out")
        o_fin = sem("o_fin"); o_sto = sem("o_sto")

        waits_ended = sem("waits_ended")
        LN1_STEPS = 4
        ROUTE_STEPS = 21

        def apart(engine):
            engine.sem_inc(waits_ended, 1)

        block = keep.enter_context(nc.Block())

        @block.sync
        def _(sp):
            for g in range(NG):
                sp.dma_start(X[:, g * GT:(g + 1) * GT, :], x_in[:, g * GT:(g + 1) * GT, :]).then_inc(x_loaded[g], 16)
                if g == 0:
                    sp.dma_start(td[:, :], decay).then_inc(small_loaded, 16)
                    sp.dma_start(tf[:, :], first).then_inc(small_loaded, 16)
                    sp.dma_start(gk[:, :, :], gate).then_inc(small_loaded, 16)
                if g == 1:
                    sp.dma_start(V[:, :, :], v_in[:, 0:GT, :]).then_inc(v_loaded, 16)
            sp.wait_ge(blank_made, 2)
            sp.dma_start(table.rearrange("(p n) w -> p n w", p=P), blank[:, :, :]).then_inc(table_blank, 16)
            for m in range(3):
                sp.dma_start(raw[:, m, :, :], weights[m][0]).then_inc(raw_loaded[m], 16)

            def store(b):
                for j in range(GT):
                    t = b * GT + j
                    sp.wait_ge(x1_made, t + 5)
                    sp.dma_start(out_rows[bass.ds(t * P, P), :], X[:, t, :]).then_inc(x1_stored, 16)
                for j in range(GT):
                    t = b * GT + j
                    sp.wait_ge(xn_made, t + 1)
                    sp.dma_start(xn_rows[bass.ds(t * P, P), :], XN[:, j, :]).then_inc(xn_stored[j], 16)
                for j in range(GT):
                    sp.wait_ge(xn_stored[j], b * 16 + 16)
                sp.sem_inc(xn_free, 1)

            sp.wait_ge(v_turned, NC)
            sp.dma_start(V[:, :, :], v_in[:, GT:2 * GT, :]).then_inc(v_loaded, 16)
            with sp.Fori(1, NG - 1) as s:
                sp.wait_ge(v_turned, (s + 1) * NC)
                sp.dma_start(V[:, :, :], v_in[:, bass.ds((s + 1) * GT, GT), :]).then_inc(v_loaded, 16)
                store(s - 1)
            store(NG - 2)
            store(NG - 1)
            sp.wait_ge(rec_stored, 16 * 2 * GT * (NG + 1))
            sp.wait_ge(x1_stored, 16 * NT)
            sp.sem_inc(phase_a_done, 1)
            sp.dma_start(lists[:, 0:EX * JT, :].rearrange("p (e j) w -> p e (j w)", e=EX),
                         table.rearrange("(e p j) w -> p e (j w)", e=EX, p=P)).then_inc(lists_loaded, 16)
            sp.wait_ge(xh_made, FT)
            with sp.Fori(1, EX) as e:
                for m in range(3):
                    sp.wait_ge(wl_made, (e - 1) * 3 * NK + NK * (m + 1))
                    sp.dma_start(raw[:, m, :, :], weights[m][e]).then_inc(raw_loaded[m], 16)
            sp.wait_ge(over_ready, 1)
            over = sp.value_load(tiles_over[0:1, 0:1], min_val=0, max_val=OV)
            with sp.If(over > 0):
                with sp.Fori(0, OV) as k:
                    sp.wait_ge(o_fin, k + 1)
                    e = sp.value_load(over_expert[0:1, bass.ds(k, 1)], min_val=0, max_val=EX - 1)
                    for m in range(3):
                        sp.dma_start(raw[:, m, :, :], weights[m][e]).then_inc(o_w, 16)

        @block.gpsimd
        def _(pool):
            for s_, n in ((f2_made, 2), (vs_made, 2), (b_scanned, 2), (den_made, 2),
                          (first_made, 2), (y_made, 4), (y_turned, 1), (x1_made, 4), (xnt_made, 2), (xn_free, 1),
                          (gated, 2), (ranks_read, 1), (xg_turned, 2), (xl_made, 2), (silu_made, 2),
                          (hm_made, 2), (out_done, 1), (fin_made, 2), (o_fin, 1)):
                pool.sem_inc(s_, n)
            pool.memset(ident[:, :], 0.0).then_inc(ident_made, 1)
            pool.wait_ge(ident_made, 1)
            pool.affine_select(out=ident[:, :], in_=ident[:, :], compare_op=ALU.not_equal, fill=1.0, base=0,
                               pattern=[[-1, P]], channel_multiplier=1).then_inc(ident_made, 1)
            pool.memset(before[:, :], 1.0).then_inc(const_made, 1)
            pool.memset(ones[:, :], 1.0)
            pool.memset(blank[:, :, 0], OOB).then_inc(blank_made, 1)
            pool.memset(blank[:, :, 1], 0).then_inc(blank_made, 1)
            pool.memset(lists[:, EX * JT, 0:1], OOB)
            pool.memset(lists[:, EX * JT, 1:2], 0)
            pool.memset(row[:, :, :], EX * NTOK).then_inc(row_init, 1)
            pool.memset(rec[:, :, :, :], 0).then_inc(row_init, 1)
            pool.memset(cum[:, 0, :], 0.0)
            pool.memset(xg[:, :, :], 0.0).then_inc(b_cleared, 1)
            pool.memset(acc[:, :, :], 0.0).then_inc(b_cleared, 1)
            pool.iota(tok[:, :], [[P, NT]], base=0, channel_multiplier=1)
            pool.iota(over_iota[:, :], [[1, OV]], base=0, channel_multiplier=0, allow_small_or_imprecise_dtypes=True)
            pool.memset(ones8[:, :], 1.0)
            pool.iota(iota8[:, :], [[1, EX]], base=0, channel_multiplier=0, allow_small_or_imprecise_dtypes=True)
            pool.wait_ge(const_made, 1)
            pool.affine_select(out=before[:, :], in_=before[:, :], compare_op=ALU.is_gt, fill=0.0, base=0,
                               pattern=[[1, P]], channel_multiplier=-1).then_inc(const_made, 1)
            pool.wait_ge(table_blank, 16)

            def store_entries(n):
                for i in n:
                    j, c = i // 2, i % 2
                    pool.indirect_dma_start(table, bass.IndirectOffsetOnAxis(ap=row[:, j, c:c + 1], axis=0),
                                            rec[:, j, c, :], None, bounds_check=last_entry,
                                            oob_is_err=False).then_inc(rec_stored, 16)

            last_entry, last_token = pool.to_reg(EX * NTOK - 1), pool.to_reg(NTOK - 1)

            def first_steps(s, c):
                if c == 0:
                    pool.wait_ge(y_turned, s * GT + 1)
                apart(pool)
                pool.tensor_copy(Y[:, c, 0:GW:T], vs[:, c % 2, 0:GW:T]).then_inc(first_made, 1)

            def unit(s, c):
                un = s * NC + c
                vb, fb, gb = vs[:, c % 2, :], f2[:, c, :], g2[:, c % 2, :]
                pool.wait_ge(vs_made, un + 3)
                pool.wait_ge(f2_made, un + 3)
                pool.wait_ge(y_made, un + 3)
                pool.tensor_tensor(gb, fb, vb, ALU.mult).then_inc(g2_made, 1)
                pool.wait_ge(b_scanned, un + 3)
                fv = fb.rearrange("p (b t) -> p b t", t=T)[:, :, 1:T]
                sv = st_b[:, c % 2, :].rearrange("p (b t) -> p b t", t=T)[:, :, 1:T]
                pool.wait_ge(g2_made, un + 1)
                pool.tensor_tensor(fv, fv, sv, ALU.add).then_inc(den_made, 1)

            def group(s, stores, more):
                first_steps(s, 0)
                first_steps(s, 1)
                if stores:
                    pool.wait_ge(row_init, 2)
                    pool.wait_ge(rows_made, s)
                    apart(pool)
                    store_entries(range(0, 3))
                unit(s, 2)
                first_steps(s, 2)
                if stores:
                    store_entries(range(3, 6))
                unit(s, 3)
                first_steps(s, 3)
                if stores:
                    store_entries(range(6, 2 * GT))
                if more:
                    unit(s + 1, 0)
                    unit(s + 1, 1)

            unit(0, 0)
            unit(0, 1)
            group(0, False, True)
            with pool.Fori(1, NG - 1) as s:
                group(s, True, True)
            group(NG - 1, True, False)
            for g in (NG - 2, NG - 1):
                pool.wait_ge(rows_made, g + 2)
                apart(pool)
                store_entries(range(2 * GT))

            pool.wait_ge(b_cleared, 2)
            pool.wait_ge(lists_loaded, 16)
            lists_e = lists[:, 0:EX * JT, :].rearrange("p (e j) w -> p e j w", e=EX)

            def gather_x(p, i):
                r, j = i // CT, i % CT
                if j == 0:
                    pool.tensor_copy(idx[:, r, :], lists_e[:, p * 2 + r, 0:CT, 0]).then_inc(idx_made, 1)
                    pool.wait_ge(idx_made, p * 2 + r + 1)
                pool.wait_ge(xg_turned, p * 2 * CT + i + 1)
                apart(pool)
                pool.indirect_dma_start(xg[:, i % 2, :], None, xn_rows,
                                        bass.IndirectOffsetOnAxis(ap=idx[:, r, j:j + 1], axis=0),
                                        bounds_check=last_token, oob_is_err=False).then_inc(xg_loaded[i % 2], 16)

            def expert(p, r, last):
                e = p * 2 + r
                nxt = [(p, CT + j) if r == 0 else (p + 1, j) for j in range(CT)]
                if not last:
                    gather_x(*nxt[0])
                    gather_x(*nxt[1])
                apart(pool)
                for j in range(CT):
                    pool.indirect_dma_start(acc[:, j, :], None, out_rows,
                                            bass.IndirectOffsetOnAxis(ap=idx[:, r, j:j + 1], axis=0),
                                            bounds_check=last_token, oob_is_err=False).then_inc(acc_loaded[j], 16)
                if not last:
                    gather_x(*nxt[2])
                    gather_x(*nxt[3])
                for j in range(CT):
                    pool.wait_ge(fin_made, e * CT + j + 3)
                    apart(pool)
                    pool.indirect_dma_start(out_rows, bass.IndirectOffsetOnAxis(ap=idx[:, r, j:j + 1], axis=0),
                                            acc[:, j, :], None, bounds_check=last_token,
                                            oob_is_err=False).then_inc(acc_stored[j], 16)
                if not last:
                    gather_x(*nxt[4])
                for j in range(CT):
                    pool.wait_ge(acc_stored[j], (e + 1) * 16)

            for j in range(CT):
                gather_x(0, j)
            with pool.Fori(0, EX // 2 - 1) as p:
                expert(p, 0, False)
                expert(p, 1, False)
            expert(EX // 2 - 1, 0, False)
            expert(EX // 2 - 1, 1, True)

            pool.wait_ge(over_ready, 1)
            over = pool.value_load(tiles_over[0:1, 0:1], min_val=0, max_val=OV)
            with pool.If(over > 0):
                with pool.Fori(0, OV) as k:
                    pool.wait_ge(o_fin, k + 1)
                    col = pool.value_load(over_column[0:1, bass.ds(k, 1)], min_val=0, max_val=EX * JT)
                    pool.tensor_copy(o_idx[:, :], lists[:, col, :]).then_inc(o_copied, 1)
                    pool.memset(o_x[:, :], 0.0).then_inc(o_copied, 1)
                    pool.memset(o_acc[:, :], 0.0).then_inc(o_copied, 1)
                    pool.wait_ge(o_copied, k * 3 + 3)
                    apart(pool)
                    for dst, src, s_ in ((o_x, xn_rows, o_xin), (o_acc, out_rows, o_ain)):
                        pool.indirect_dma_start(dst[:, :], None, src,
                                                bass.IndirectOffsetOnAxis(ap=o_idx[:, 0:1], axis=0),
                                                bounds_check=last_token, oob_is_err=False).then_inc(s_, 16)
                    pool.wait_ge(o_fin, k + 2)
                    apart(pool)
                    pool.indirect_dma_start(out_rows, bass.IndirectOffsetOnAxis(ap=o_idx[:, 0:1], axis=0),
                                            o_r[:, :], None, bounds_check=last_token,
                                            oob_is_err=False).then_inc(o_sto, 16)
                    pool.wait_ge(o_sto, k * 16 + 16)

        @block.scalar
        def _(act):
            act.add_instruction(mybir.InstLoadActFuncSet(name=nc.get_next_instruction_name(),
                                                         act_func_set_id=EXP_LN_SET))
            act.wait_ge(small_loaded, 48)
            act.activation(etd[:, :], td[:, :], ACT.Exp).then_inc(decay_exp, 1)
            act.wait_ge(decay_exp, 1)
            act.activation(dd[:, :], etd[:, :], ACT.Exp, scale=-1.0).then_inc(decay_exp, 1)

            def first_inv_sqrt(start, log, v, n):
                act.wait_ge(ln1, n * (LN1_STEPS + 2) + 1)
                act.activation(log, v, ACT.Ln).then_inc(ln1_act, 1)
                act.wait_ge(ln1_act, n * 2 + 1)
                act.activation(start, log, ACT.Exp, scale=-0.5).then_inc(ln1_act, 1)

            def exponentials(s, c):
                un = s * NC + c
                act.wait_ge(k_turned, un + 1)
                act.wait_ge(b_scanned, un + 1)
                act.activation(f1[:, c % 2, :], bank[c % 2][:, :], ACT.Exp, bias=ub1[:, c:c + 1])
                act.wait_ge(y_made, un + 1)
                act.activation(f2[:, c, :], bank[c % 2][:, :], ACT.Exp, bias=ub2[:, c:c + 1]).then_inc(f2_made, 1)
                act.wait_ge(v_turned, un + 1)
                act.wait_ge(first_made, un + 1)
                act.activation(vs[:, c % 2, :], bank[2 + c % 2][:, :], ACT.Copy).then_inc(vs_made, 1)

            def inverse(s, c):
                un = s * NC + c
                fv = f2[:, c, :].rearrange("p (b t) -> p b t", t=T)[:, :, 1:T]
                act.wait_ge(den_made, un + 3)
                act.activation(fv, fv, ACT.Ln).then_inc(ln_made, 1)
                act.wait_ge(ln_made, un + 1)
                act.activation(fv, fv, ACT.Exp, scale=-1.0).then_inc(rden_made, 1)

            def normalise(g):
                for j in range(GT):
                    t = g * GT + j
                    act.activation(K[:, j, :], X[:, t, :], ACT.Identity, bias=nm1[:, bass.ds(t, 1)],
                                   scale=rs1[:, bass.ds(t, 1)]).then_inc(k_ready, 1)

            def normalised(b):
                act.wait_ge(xn_free, b + 1)
                act.wait_ge(ln2, (b + 1) * (LN1_STEPS + 2))
                for j in range(GT):
                    act.activation(XN[:, j, :], X[:, b * GT + j, :], ACT.Identity, bias=nm2[:, j:j + 1],
                                   scale=rs2[:, j:j + 1]).then_inc(xn_made, 1)

            def turned_norm(b, tiles):
                for j in tiles:
                    t = b * GT + j
                    act.wait_ge(xn_turned, t + 1)
                    act.wait_ge(gated, t + 1)
                    act.activation(XNT[:, j % 2, :, :], bank[4 + j % 2].rearrange("p (k n) -> p k n", n=P),
                                   ACT.Copy).then_inc(xnt_made, 1)

            def group(s, front, back, more):
                b = s - 1
                if front:
                    inverse(s, 0)
                    inverse(s, 1)
                    exponentials(s, 2)
                if not back:
                    act.wait_ge(ln1, 2 * (LN1_STEPS + 2))
                if more:
                    act.wait_ge(k_turned, (s + 1) * NC)
                    normalise(s + 1)
                if back:
                    act.wait_ge(ln2, b * (LN1_STEPS + 2) + 1)
                    act.activation(lnv2[:, :], ve2[:, :], ACT.Ln).then_inc(ln2_act, 1)
                    act.wait_ge(ln2_act, b * 2 + 1)
                    act.activation(q0[:, :], lnv2[:, :], ACT.Exp, scale=-0.5).then_inc(ln2_act, 1)
                if front:
                    exponentials(s, 3)
                if front:
                    inverse(s, 2)
                if back:
                    normalised(b)
                if more:
                    exponentials(s + 1, 0)
                if back:
                    turned_norm(b, (0, 1))
                if front:
                    inverse(s, 3)
                if more:
                    exponentials(s + 1, 1)
                if back:
                    turned_norm(b, (2, 3))
                if back:
                    act.wait_ge(delta_made, b + 1)
                    act.activation(e2[:, :], dlt[:, :], ACT.Exp).then_inc(e2_made, 1)

            first_inv_sqrt(r0[:, 0:GT], lnv[:, 0:GT], ve[:, 0:GT], 0)
            act.wait_ge(ln1, LN1_STEPS + 2)
            normalise(0)
            exponentials(0, 0)
            exponentials(0, 1)
            first_inv_sqrt(r0[:, GT:NT], lnv[:, GT:NT], ve[:, GT:NT], 1)
            group(0, True, False, True)
            with act.Fori(1, NG - 1) as s:
                group(s, True, True, True)
            group(NG - 1, True, True, False)
            group(NG, False, True, False)
            for n in range(3 * NK):
                if n % NK == 0:
                    act.wait_ge(raw_loaded[n // NK], 16)
                act.activation(wh[0][:, n // NK, n % NK, :], raw[:, n // NK, n % NK, :], ACT.Copy).then_inc(wh_made, 1)
            act.wait_ge(e2_made, NG)
            act.sem_inc(phase_a_done, 1)

            act.wait_ge(phase_a_done, 4)

            def x_high(p, i):
                r, j, tt = i // CT, i % CT, p * 2 * CT + i
                act.wait_ge(xg_turned, tt + 3)
                act.activation(xth[r][:, :, j * P:(j + 1) * P], bank[6 + i % 2].rearrange("p (k n) -> p k n", n=P),
                               ACT.Copy).then_inc(xh_made, 1)

            def w_high(p, r, n):
                e, m = p * 2 + r, n // NK
                if n == 0:
                    act.wait_ge(out_done, e * CT + 1)
                if n % NK == 0:
                    act.wait_ge(raw_loaded[m], (e + 2) * 16)
                act.activation(wh[1 - r][:, m, n % NK, :], raw[:, m, n % NK, :], ACT.Copy).then_inc(wh_made, 1)

            def h_high(p, r, l):
                hb = (p * 2 + r) * 2 * NK + l
                act.wait_ge(hm_made, hb + 3)
                w = PARTS[l // NK]
                act.activation(hth[:, l % NK, w], hm[:, l % 2, 0:w.stop - w.start], ACT.Copy).then_inc(hh_made, 1)

            def silu(p, r, l):
                hb = (p * 2 + r) * 2 * NK + l
                act.wait_ge(h0_done, hb + 1)
                act.wait_ge(hm_made, hb + 1)
                n = PARTS[l // NK].stop - PARTS[l // NK].start
                act.activation(sl[:, l % 2, 0:n], bank[l % 2][:, 0:n], ACT.Silu).then_inc(silu_made, 1)

            def expert(p, r, last):
                nxt = [(p, CT + j) if r == 0 else (p + 1, j) for j in range(CT)]
                for l in range(2 * NK):
                    if l > 0:
                        h_high(p, r, l - 1)
                    silu(p, r, l)
                    if l in (1, 2, 3):
                        x_high(p, r * CT + l + 1)
                    if l in (6, 7) and not last:
                        x_high(*nxt[l - 6])
                    if l >= 2 and not last:
                        w_high(p, r, l - 2)
                h_high(p, r, 2 * NK - 1)
                if not last:
                    for n in range(2 * NK - 2, 3 * NK):
                        w_high(p, r, n)

            for j in range(FT):
                x_high(0, j)
            with act.Fori(0, EX // 2 - 1) as p:
                expert(p, 0, False)
                expert(p, 1, False)
            expert(EX // 2 - 1, 0, False)
            expert(EX // 2 - 1, 1, True)

            act.wait_ge(over_ready, 1)
            over = act.value_load(tiles_over[0:1, 0:1], min_val=0, max_val=OV)
            with act.If(over > 0):
                with act.Fori(0, OV) as k:
                    act.wait_ge(o_xturn, k + 1)
                    act.activation(o_xt[:, :, :], bank[6].rearrange("p (k n) -> p k n", n=P), ACT.Copy).then_inc(o_xtm, 1)
                    act.wait_ge(o_h01, k + 1)
                    act.activation(o_s[:, :], bank[0][:, :], ACT.Silu).then_inc(o_sm, 1)
                    act.wait_ge(o_hturn, k + 1)
                    act.activation(o_ht[:, :, :], bank[7].rearrange("p (k n) -> p k n", n=P), ACT.Copy).then_inc(o_htm, 1)

        @block.vector
        def _(dve):
            def inv_sqrt(v, start, a, b, c, r, sem_, base, n):
                steps = (lambda: dve.tensor_tensor(a, start, start, ALU.mult),
                         lambda: dve.tensor_tensor(b, a, v, ALU.mult),
                         lambda: dve.tensor_scalar(c, b, -0.5, 1.5, ALU.mult, ALU.add),
                         lambda: dve.tensor_tensor(r, c, start, ALU.mult))
                for i in range(len(steps)):
                    steps[i]().then_inc(sem_, 1)
                    dve.wait_ge(sem_, base + i + 1)

            dve.memset(decay_row[:, :, :], 1.0).then_inc(dve_prologue, 1)
            dve.wait_ge(small_loaded, 48)
            dve.tensor_scalar(ub1[:, :], tf[:, :], 0.0, -1.0, ALU.max, ALU.mult)
            dve.tensor_scalar(ub2[:, :], tf[:, :], 0.0, None, ALU.min)

            def ln1_stats(g):
                dve.wait_ge(x_loaded[g], 16)
                for t in range(g * GT, (g + 1) * GT):
                    dve.bn_stats(stat1[:, t, :], X[:, t, :]).then_inc(ln1_stat, 1)

            def ln1_sums(t0, t1, n):
                for t in range(t0, t1):
                    dve.wait_ge(ln1_stat, t + 1)
                    apart(dve)
                    ins = dve.bn_aggr(mv1[:, t, :], stat1[:, t, :])
                ins.then_inc(ln1_sum, 1)
                dve.wait_ge(ln1_sum, n + 1)
                dve.tensor_scalar(ve[:, t0:t1], mv1[:, t0:t1, 1], EPS, None, ALU.add).then_inc(ln1, 1)

            def ln1_finish(t0, t1, n):
                w = slice(t0, t1)
                dve.wait_ge(ln1_act, 2 * n + 2)
                dve.wait_ge(ln1, n * (LN1_STEPS + 2) + 1)
                inv_sqrt(ve[:, w], r0[:, w], na[:, w], nb[:, w], ncf[:, w], rs1[:, w], ln1,
                         n * (LN1_STEPS + 2) + 1, NT)
                dve.scalar_tensor_tensor(nm1[:, w], mv1[:, w, 0], -1.0, rs1[:, w], ALU.mult, ALU.mult).then_inc(ln1, 1)

            ln1_stats(0)
            ln1_sums(0, GT, 0)
            dve.wait_ge(decay_exp, 2)
            dve.wait_ge(dve_prologue, 1)
            for c in range(NC):
                last = dve.tensor_scalar(decay_row[:, c, :], decay_row[:, c, :], dd[:, c:c + 1], None, ALU.mult)
            last.then_inc(dve_prologue, 1)
            ln1_finish(0, GT, 0)
            dve.wait_ge(dve_prologue, 2)
            dve.memset(decay_row[:, :, T:T + 1], 0.0).then_inc(dve_prologue, 1)
            dve.wait_ge(dve_prologue, 3)
            dve.sem_inc(rows_made, 1)
            for g in range(1, NG):
                ln1_stats(g)

            def finish_y(s, c):
                un = s * NC + c
                yv, nv, rv = (z.rearrange("p (b t) -> p b t", t=T)[:, :, 1:T]
                              for z in (Y[:, c, :], g2[:, c % 2, :], f2[:, c, :]))
                dve.wait_ge(num_made, un + 1)
                dve.wait_ge(rden_made, un + 1)
                if c == 0:
                    dve.wait_ge(y_turned, s * GT + 1)
                dve.tensor_tensor(yv, nv, rv, ALU.mult).then_inc(y_made, 1)

            def scans(s, c):
                un, q = s * NC + c, c % 2
                dve.wait_ge(f2_made, un + 3)
                dve.wait_ge(vs_made, un + 3)
                dve.tensor_tensor(g1[:, q, :], f1[:, q, :], vs[:, q, :], ALU.mult).then_inc(g1_made, 1)
                dve.wait_ge(den_made, un + 1)
                dve.tensor_tensor_scan(st_b[:, q, 1:GW], decay_row[:, c, 0:GW - 1], f1[:, q, 0:GW - 1], 0.0,
                                       ALU.mult, ALU.add).then_inc(b_scanned, 1)
                dve.wait_ge(g1_made, un + 1)
                dve.tensor_tensor_scan(st_a[:, q, 1:GW], decay_row[:, c, 0:GW - 1], g1[:, q, 0:GW - 1], 0.0,
                                       ALU.mult, ALU.add).then_inc(a_scanned, 1)

            def numerator(s, c):
                un, q = s * NC + c, c % 2
                gv, av = (z.rearrange("p (b t) -> p b t", t=T)[:, :, 1:T] for z in (g2[:, q, :], st_a[:, q, :]))
                dve.wait_ge(g2_made, un + 1)
                dve.wait_ge(a_scanned, un + 1)
                dve.tensor_tensor(gv, gv, av, ALU.add).then_inc(num_made, 1)

            def w_low(h, l, r):
                return dve.tensor_tensor(l, r, h.bitcast(F32), ALU.subtract)

            def routing(s):
                n = [0]

                def step(ins):
                    n[0] += 1
                    ins.then_inc(route, 1)
                    dve.wait_ge(route, s * ROUTE_STEPS + n[0])

                dve.wait_ge(gated, s * GT + GT + 2)
                dve.wait_ge(rec_stored, (s + 1) * 16 * 2 * GT)
                step(dve.tensor_copy(lg[:, :, :], logits))
                apart(dve)
                for j in range(GT):
                    ins = dve.max(m8[:, j, :], lg[:, j, :])
                step(ins)
                apart(dve)
                for j in range(GT):
                    ins = dve.max_index(i8[:, j, :], m8[:, j, :], lg[:, j, :])
                step(ins)
                dve.tensor_tensor(dlt[:, :], m8[:, :, 1], m8[:, :, 0], ALU.subtract).then_inc(delta_made, 1)
                step(dve.tensor_copy(idxf[:, :, :], i8[:, :, 0:2]))
                step(dve.tensor_tensor(oh[:, :, :, :],
                                       iota8[:, None, None, :].to_broadcast([P, GT, 2, EX]),
                                       idxf[:, :, :, None].to_broadcast([P, GT, 2, EX]), ALU.is_equal))
                step(dve.tensor_tensor(msk[:, :, :], oh[:, :, 0, :], oh[:, :, 1, :], ALU.add))
                for j in range(GT):
                    ins = dve.tensor_tensor(cum[:, j + 1, :], cum[:, j, :], msk[:, j, :], ALU.add)
                    if j < GT - 1:
                        step(ins)
                ins.then_inc(mask_made, 1)
                step(dve.tensor_scalar(ebs[:, :, :], i8[:, :, 0:2].bitcast(I32), NTOK.bit_length() - 1, None,
                                       ALU.logical_shift_left))
                dve.wait_ge(e2_made, s + 1)
                step(dve.tensor_scalar(e2p[:, :], e2[:, :], 1.0, None, ALU.add))
                step(dve.reciprocal(p1[:, :], e2p[:, :]))
                recf = rec.bitcast(F32)
                step(dve.tensor_copy(recf[:, :, 0, 1], p1[:, :]))
                step(dve.tensor_tensor(recf[:, :, 1, 1], p1[:, :], e2[:, :], ALU.mult))
                for q in range(2):
                    ins = dve.tensor_copy(rec[:, :, q, 0], tok[:, bass.ds(s * GT, GT)])
                step(ins)
                dve.wait_ge(ranked, s + 1)
                step(dve.tensor_tensor(ohr[:, :, :, :], oh[:, :, :, :],
                                       ranks[:, :, None, :].to_broadcast([P, GT, 2, EX]), ALU.mult))
                dve.tensor_copy(cum[:, 0, :], cum[:, GT, :]).then_inc(ranks_read, 1)
                step(dve.tensor_reduce(rk[:, :, :], ohr[:, :, :, :], AX.X, ALU.add))
                step(dve.tensor_copy(rki[:, :, :], rk[:, :, :]))
                step(dve.tensor_scalar(lo7[:, :, :], rki[:, :, :], P - 1, JT.bit_length() - 1,
                                       ALU.bitwise_and, ALU.logical_shift_left))
                step(dve.tensor_scalar(hi4[:, :, :], rki[:, :, :], P.bit_length() - 1, None,
                                       ALU.logical_shift_right))
                step(dve.tensor_tensor(lh[:, :, :], lo7[:, :, :], hi4[:, :, :], ALU.bitwise_or))
                dve.tensor_tensor(row[:, :, :], lh[:, :, :], ebs[:, :, :], ALU.bitwise_or).then_inc(rows_made, 1)
                assert n[0] == ROUTE_STEPS, n[0]

            dve.wait_ge(const_made, 2)

            def residual(b, tiles):
                for j in tiles:
                    t = b * GT + j
                    dve.wait_ge(y_turned, t + 2)
                    dve.tensor_tensor(X[:, t, :], X[:, t, :], bank[4 + j][:, :], ALU.add).then_inc(x1_made, 1)
                    if j % 2:
                        for i in (j - 1, j):
                            dve.wait_ge(x1_made, b * GT + i + 5)
                            apart(dve)
                            dve.bn_stats(stat2[:, i, :], X[:, b * GT + i, :]).then_inc(stat2_made, 1)

            def ln2_sums(b):
                for j in range(GT):
                    dve.wait_ge(stat2_made, b * GT + j + 1)
                    apart(dve)
                    ins = dve.bn_aggr(mv2[:, j, :], stat2[:, j, :])
                ins.then_inc(mv2_made, 1)
                dve.wait_ge(mv2_made, b + 1)
                dve.tensor_scalar(ve2[:, :], mv2[:, :, 1], EPS, None, ALU.add).then_inc(ln2, 1)

            def ln2_finish(b):
                dve.wait_ge(ln2_act, b * 2 + 2)
                dve.wait_ge(ln2, b * (LN1_STEPS + 2) + 1)
                inv_sqrt(ve2[:, :], q0[:, :], qa[:, :], qb[:, :], qc[:, :], rs2[:, :], ln2,
                         b * (LN1_STEPS + 2) + 1, GT)
                dve.scalar_tensor_tensor(nm2[:, :], mv2[:, :, 0], -1.0, rs2[:, :], ALU.mult, ALU.mult).then_inc(ln2, 1)

            def group(s, front, back, more):
                b = s - 1
                if back:
                    residual(b, (0, 1))
                if front:
                    finish_y(s, 0)
                    numerator(s, 1)
                if back:
                    residual(b, (2, 3))
                    ln2_sums(b)
                if front:
                    scans(s, 2)
                    finish_y(s, 1)
                    numerator(s, 2)
                if back:
                    ln2_finish(b)
                if front:
                    scans(s, 3)
                    finish_y(s, 2)
                    numerator(s, 3)
                if more:
                    scans(s + 1, 0)
                if front:
                    finish_y(s, 3)
                if more:
                    numerator(s + 1, 0)
                    scans(s + 1, 1)
                if back:
                    routing(b)

            scans(0, 0)
            numerator(0, 0)
            scans(0, 1)
            ln1_sums(GT, NT, 1)
            ln1_finish(GT, NT, 1)
            group(0, True, False, True)
            with dve.Fori(1, NG - 1) as s:
                group(s, True, True, True)
            group(NG - 1, True, True, False)
            group(NG, False, True, False)
            dve.wait_ge(rows_made, NG + 1)
            dve.wait_ge(totals_made, 1)
            dve.tensor_copy(totals[:, :], bank[6][:, 128:128 + EX]).then_inc(over_made, 1)
            dve.wait_ge(over_made, 1)
            dve.sem_inc(phase_a_done, 1)
            for n in range(3 * NK):
                m, k = n // NK, n % NK
                dve.wait_ge(wh_made, n + 1)
                w_low(wh[0][:, m, k, :], wl[0][:, m, k, :], raw[:, m, k, :]).then_inc(wl_made, 1)

            dve.wait_ge(phase_a_done, 4)

            def x_low(p, i):
                r, j, tt = i // CT, i % CT, p * 2 * CT + i
                dve.wait_ge(xh_made, tt + 1)
                dve.tensor_tensor(xtl[r][:, :, j * P:(j + 1) * P], bank[6 + i % 2].rearrange("p (k n) -> p k n", n=P),
                                  xth[r][:, :, j * P:(j + 1) * P].bitcast(F32), ALU.subtract).then_inc(xl_made, 1)

            def wl_chunk(p, r, n):
                e, m = p * 2 + r, n // NK
                dve.wait_ge(wh_made, (e + 1) * 3 * NK + n + 1)
                w_low(wh[1 - r][:, m, n % NK, :], wl[1 - r][:, m, n % NK, :], raw[:, m, n % NK, :]).then_inc(wl_made, 1)

            def h_low(p, r, l):
                hb = (p * 2 + r) * 2 * NK + l
                w = PARTS[l // NK]
                dve.wait_ge(hh_made, hb + 1)
                dve.tensor_tensor(htl[:, l % NK, w], hm[:, l % 2, 0:w.stop - w.start], hth[:, l % NK, w].bitcast(F32),
                                  ALU.subtract).then_inc(hl_made, 1)

            def gated_product(p, r, l):
                hb = (p * 2 + r) * 2 * NK + l
                dve.wait_ge(silu_made, hb + 3)
                dve.wait_ge(h1_done, hb + 1)
                n = PARTS[l // NK].stop - PARTS[l // NK].start
                dve.tensor_tensor(hm[:, l % 2, 0:n], bank[2 + l % 2][:, 0:n], sl[:, l % 2, 0:n],
                                  ALU.mult).then_inc(hm_made, 1)

            listf = lists.bitcast(F32)

            def finish(p, r, j):
                e = p * 2 + r
                tt = e * CT + j
                dve.wait_ge(out_done, tt + 2)
                dve.wait_ge(acc_loaded[j], (e + 1) * 16)
                dve.scalar_tensor_tensor(acc[:, j, :], bank[4 + (r * CT + j) % 2][:, :],
                                         listf[:, e * JT + j, 1:2], acc[:, j, :],
                                         ALU.mult, ALU.add).then_inc(fin_made, 1)

            def expert(p, r, last):
                nxt = [(p, CT + j) if r == 0 else (p + 1, j) for j in range(CT)]
                for l in range(2 * NK):
                    if l > 0:
                        h_low(p, r, l - 1)
                    if l in (1, 2, 3):
                        x_low(p, r * CT + l + 1)
                    if l in (6, 7) and not last:
                        x_low(*nxt[l - 6])
                    if l >= 2 and not last:
                        wl_chunk(p, r, l - 2)
                    gated_product(p, r, l)
                h_low(p, r, 2 * NK - 1)
                for j in range(CT):
                    if not last:
                        for n in range(2 * NK - 2, 3 * NK)[j + (j > 0):j + 2]:
                            wl_chunk(p, r, n)
                    finish(p, r, j)

            for j in range(FT):
                x_low(0, j)
            dve.wait_ge(lists_loaded, 16)
            with dve.Fori(0, EX // 2 - 1) as p:
                expert(p, 0, False)
                expert(p, 1, False)
            expert(EX // 2 - 1, 0, False)
            expert(EX // 2 - 1, 1, True)

            n = [1]

            def step(ins):
                n[0] += 1
                ins.then_inc(over_made, 1)
                dve.wait_ge(over_made, n[0])

            step(dve.tensor_scalar(cnt_f[:, :], totals[:, :], float(P - 1), None, ALU.add))
            step(dve.tensor_copy(cnt_b[:, :], cnt_f[:, :]))
            step(dve.tensor_scalar(cnt_t[:, :], cnt_b[:, :], P.bit_length() - 1, None, ALU.logical_shift_right))
            step(dve.tensor_copy(cnt_f[:, :], cnt_t[:, :]))
            step(dve.tensor_scalar(extra[:, :], cnt_f[:, :], -float(CT), 0.0, ALU.add, ALU.max))
            step(dve.tensor_tensor_scan(extra_sum[:, :], ones8[:, :], extra[:, :], 0.0, ALU.mult, ALU.add))
            step(dve.tensor_copy(tiles_over[:, :], extra_sum[:, EX - 1:EX]))
            step(dve.tensor_tensor(past[:, :, :], over_iota[:, :, None].to_broadcast([P, OV, EX]),
                                   extra_sum[:, None, :].to_broadcast([P, OV, EX]), ALU.is_ge))
            step(dve.tensor_tensor(past_n[:, :, :], past[:, :, :],
                                   extra[:, None, :].to_broadcast([P, OV, EX]), ALU.mult))
            step(dve.tensor_reduce(past_experts[:, :], past[:, :, :], AX.X, ALU.add))
            step(dve.tensor_reduce(past_tiles[:, :], past_n[:, :, :], AX.X, ALU.add))
            step(dve.tensor_tensor(over_j[:, :], over_iota[:, :], past_tiles[:, :], ALU.subtract))
            step(dve.scalar_tensor_tensor(over_c[:, :], past_experts[:, :], float(JT), over_j[:, :],
                                          ALU.mult, ALU.add))
            step(dve.tensor_scalar(over_d[:, :], over_c[:, :], float(CT), float(EX * JT), ALU.add, ALU.min))
            step(dve.tensor_copy(over_column[:, :], over_d[:, :]))
            step(dve.tensor_scalar(over_j[:, :], past_experts[:, :], float(EX - 1), None, ALU.min))
            step(dve.tensor_copy(over_expert[:, :], over_j[:, :]))
            dve.sem_inc(over_ready, 1)
            over = dve.value_load(tiles_over[0:1, 0:1], min_val=0, max_val=OV)
            with dve.If(over > 0):
                with dve.Fori(0, OV) as k:
                    dve.wait_ge(o_sm, k + 1)
                    dve.wait_ge(o_h01, k + 1)
                    dve.wait_ge(o_copied, k * 3 + 3)
                    dve.tensor_tensor(o_h[:, :], bank[2][:, :], o_s[:, :], ALU.mult).then_inc(o_hm, 1)
                    dve.wait_ge(o_out, k + 1)
                    dve.wait_ge(o_ain, k * 16 + 16)
                    dve.scalar_tensor_tensor(o_r[:, :], bank[4][:, :], o_idx.bitcast(F32)[:, 1:2], o_acc[:, :],
                                             ALU.mult, ALU.add).then_inc(o_fin, 1)

        @block.tensor
        def _(pe):
            pe.wait_ge(ident_made, 2)
            pe.wait_ge(const_made, 2)
            pe.wait_ge(small_loaded, 48)

            def turn_kv(s, c):
                un = s * NC + c
                ch = slice(c * P, (c + 1) * P)
                if c == 0:
                    pe.wait_ge(k_ready, s * GT + GT)
                pe.wait_ge(f2_made, un + 1)
                for j in range(GT):
                    ins = pe.transpose(bank[c % 2][:, j * P:(j + 1) * P], K[:, j, ch], ident[:, :])
                ins.then_inc(k_turned, 1)
                if c == 0:
                    pe.wait_ge(v_loaded, s * 16 + 16)
                pe.wait_ge(vs_made, un + 1)
                for j in range(GT):
                    ins = pe.transpose(bank[2 + c % 2][:, j * P:(j + 1) * P], V[:, j, ch], ident[:, :])
                ins.then_inc(v_turned, 1)

            def turn_y(b):
                pe.wait_ge(y_made, b * NC + NC + 4)
                pe.wait_ge(first_made, b * NC + NC + 2)
                pe.wait_ge(xnt_made, b * GT + 2)
                pe.wait_ge(ranks_read, b + 1)
                for j in range(GT):
                    pe.wait_ge(x1_made, b * GT + j + 1)
                    for c in range(NC):
                        ins = pe.transpose(bank[4 + j][:, c * P:(c + 1) * P], Y[:, c, j * P:(j + 1) * P],
                                           ident[:, :])
                    ins.then_inc(y_turned, 1)

            def turn_norm(b, j):
                t = b * GT + j
                pe.wait_ge(xn_made, t + 1)
                pe.wait_ge(xnt_made, t + 1)
                pe.wait_ge(x1_made, b * GT + GT + 4)
                for c in range(NC):
                    ins = pe.transpose(bank[4 + j % 2][:, c * P:(c + 1) * P], XN[:, j, c * P:(c + 1) * P], ident[:, :])
                ins.then_inc(xn_turned, 1)

            def router(b, j):
                pe.wait_ge(xnt_made, b * GT + j + 3)
                for c in range(NC):
                    ins = pe.matmul(logits[:, j, :], XNT[:, j % 2, c, :], gk[:, c, :],
                                    start=(c == 0), stop=(c == NC - 1))
                ins.then_inc(gated, 1)

            def group(s, front, back, more):
                b = s - 1
                if back:
                    turn_y(b)
                if front:
                    turn_kv(s, 2)
                    turn_kv(s, 3)
                if more:
                    turn_kv(s + 1, 0)
                if back:
                    turn_norm(b, 0)
                    turn_norm(b, 1)
                    router(b, 0)
                    router(b, 1)
                if more:
                    turn_kv(s + 1, 1)
                if back:
                    turn_norm(b, 2)
                    turn_norm(b, 3)
                    router(b, 2)
                    router(b, 3)
                if back:
                    pe.wait_ge(mask_made, b + 1)
                    pe.matmul(ranks, before[:, :], msk[:, :, :], start=True, stop=False)
                    pe.matmul(ranks, ones[:, :], cum[:, 0:GT, :], start=False, stop=True).then_inc(ranked, 1)

            turn_kv(0, 0)
            turn_kv(0, 1)
            group(0, True, False, True)
            with pe.Fori(1, NG - 1) as s:
                group(s, True, True, True)
            group(NG - 1, True, True, False)
            group(NG, False, True, False)
            pe.wait_ge(ranks_read, NG + 1)
            pe.matmul(bank[6][:, 128:128 + EX], ones[:, :], cum[:, 0, :], start=True, stop=True).then_inc(totals_made, 1)
            pe.wait_ge(totals_made, 1)
            pe.sem_inc(phase_a_done, 1)

            pe.wait_ge(over_made, 1)

            def turn_x(p, i):
                tt = p * 2 * CT + i
                pe.wait_ge(xg_loaded[i % 2], (p * CT + i // 2 + 1) * 16)
                pe.wait_ge(xl_made, tt + 1)
                for c in range(NK):
                    ins = pe.transpose(bank[6 + i % 2][:, c * P:(c + 1) * P], xg[:, i % 2, c * P:(c + 1) * P],
                                       ident[:, :])
                ins.then_inc(xg_turned, 1)

            def split_product(dst, parts):
                terms = [t for lh_, ll_, rh_, rl_ in parts for t in ((lh_, rh_), (lh_, rl_), (ll_, rh_))]
                for i, (a, b_) in enumerate(terms):
                    ins = pe.matmul(dst, a, b_, start=(i == 0), stop=(i == len(terms) - 1))
                return ins

            def hidden(p, r, l):
                e, half, mb = p * 2 + r, l // NK, l % NK
                hb = e * 2 * NK + l
                w, mc = PARTS[half], slice(mb * P, (mb + 1) * P)
                if l == 0:
                    pe.wait_ge(wl_made, e * 3 * NK + NK)
                    pe.wait_ge(xl_made, e * CT + FT + 2)
                if l == NK:
                    pe.wait_ge(xl_made, e * CT + CT + 2)
                for m, free, done in ((0, silu_made, h0_done), (1, hm_made, h1_done)):
                    if l == 0 and m == 1:
                        pe.wait_ge(wl_made, e * 3 * NK + 2 * NK)
                    pe.wait_ge(free, hb + 1)
                    split_product(bank[2 * m + l % 2][:, 0:w.stop - w.start],
                                  [(wh[r][:, m, k, mc], wl[r][:, m, k, mc], xth[r][:, k, w], xtl[r][:, k, w])
                                   for k in range(NK)]).then_inc(done, 1)

            def output(p, r, j):
                e = p * 2 + r
                tw = slice(j * P, (j + 1) * P)
                if j == 0:
                    pe.wait_ge(wl_made, (e + 1) * 3 * NK)
                pe.wait_ge(hl_made, e * 2 * NK + (NK if j < FT else 2 * NK))
                pe.wait_ge(fin_made, e * CT + j + 1)
                split_product(bank[4 + (r * CT + j) % 2][:, :],
                              [(hth[:, k, tw], htl[:, k, tw], wh[r][:, 2, k, :], wl[r][:, 2, k, :])
                               for k in range(NK)]).then_inc(out_done, 1)

            def expert(p, r, last):
                nxt = [(p, CT + j) if r == 0 else (p + 1, j) for j in range(CT)]
                for l in range(2 * NK):
                    hidden(p, r, l)
                    if l in (0, 1, 2):
                        turn_x(p, r * CT + l + 2)
                    if l in (5, 6) and not last:
                        turn_x(*nxt[l - 5])
                for j in range(CT):
                    output(p, r, j)

            for j in range(FT):
                turn_x(0, j)
            with pe.Fori(0, EX // 2 - 1) as p:
                expert(p, 0, False)
                expert(p, 1, False)
            expert(EX // 2 - 1, 0, False)
            expert(EX // 2 - 1, 1, True)

            pe.wait_ge(fin_made, EX * CT + 2)
            pe.wait_ge(over_ready, 1)
            over = pe.value_load(tiles_over[0:1, 0:1], min_val=0, max_val=OV)
            with pe.If(over > 0):
                with pe.Fori(0, OV) as k:
                    pe.wait_ge(o_xin, k * 16 + 16)
                    for c in range(NK):
                        ins = pe.transpose(bank[6][:, c * P:(c + 1) * P], o_x[:, c * P:(c + 1) * P], ident[:, :])
                    ins.then_inc(o_xturn, 1)
                    pe.wait_ge(o_xtm, k + 1)
                    pe.wait_ge(o_w, k * 48 + 48)
                    for m in range(2):
                        for c in range(NK):
                            ins = pe.matmul(bank[2 * m][:, :], o_xt[:, c, :], raw[:, m, c, :],
                                            start=(c == 0), stop=(c == NK - 1))
                    ins.then_inc(o_h01, 1)
                    pe.wait_ge(o_hm, k + 1)
                    for c in range(NK):
                        ins = pe.transpose(bank[7][:, c * P:(c + 1) * P], o_h[:, c * P:(c + 1) * P], ident[:, :])
                    ins.then_inc(o_hturn, 1)
                    pe.wait_ge(o_htm, k + 1)
                    for c in range(NK):
                        ins = pe.matmul(bank[4][:, :], o_ht[:, c, :], raw[:, 2, c, :],
                                        start=(c == 0), stop=(c == NK - 1))
                    ins.then_inc(o_out, 1)


def kernel(x, ctx_2048, L0_xattn_time_decay, L0_xattn_time_first, L0_ffn_gate_kernel,
           L0_ffn_wi_0, L0_ffn_wi_1, L0_ffn_wo):
    import numpy as np
    import concourse.bacc as bacc
    from concourse.bass_utils import run_bass_kernel_spmd

    nc = bacc.Bacc("TRN2", target_bir_lowering=False, num_devices=1)
    arrays = {
        "in_x": np.ascontiguousarray(x),
        "in_ctx": np.ascontiguousarray(ctx_2048),
        "in_decay": np.ascontiguousarray(np.asarray(L0_xattn_time_decay).reshape(NC, P).T),
        "in_first": np.ascontiguousarray(np.asarray(L0_xattn_time_first).reshape(NC, P).T),
        "in_gate": np.ascontiguousarray(np.asarray(L0_ffn_gate_kernel).reshape(NC, P, EX).transpose(1, 0, 2)),
        "in_wi0": np.ascontiguousarray(L0_ffn_wi_0),
        "in_wi1": np.ascontiguousarray(L0_ffn_wi_1),
        "in_wo": np.ascontiguousarray(L0_ffn_wo),
    }
    args = [nc.dram_tensor(n, a.shape, mybir.dt.from_np(a.dtype), kind="ExternalInput").ap()
            for n, a in arrays.items()]
    out = nc.dram_tensor("out_x", (B, T, C), F32, kind="ExternalOutput").ap()
    build(nc, *args, out)
    r = run_bass_kernel_spmd(nc, [arrays], core_ids=[0])
    return r.results[0]["out_x"]
```

```python
from contextlib import ExitStack

import concourse.bass as bass
from concourse import mybir

P = 128
B, T, C = 8, 256, 512
NTOK = B * T
NT = NTOK // P
NC = C // P
GT = 4
NG = NT // GT
GW = GT * P
EX, M = 8, 512
NK = C // P
EPS = 1e-5
EXP_LN_SET = 6
CT = 5
CAP = CT * P
FT = CT // 2
PARTS = (slice(0, FT * P), slice(FT * P, CAP))
SHORT, SHORTER = CAP - P // 2, CAP - P
JT = NT
OOB = NTOK
OV = max(n * min(JT - CT, JT) if 2 * n <= 4 else (2 * NTOK + n * (P - 1)) // P - CT * n
         for n in range(1, EX + 1) if n <= 2 or (2 * NTOK + n * (P - 1)) // P - CT * n > 0)

F32, F32R = mybir.dt.float32, mybir.dt.float32r
BF16, I32, U32 = mybir.dt.bfloat16, mybir.dt.int32, mybir.dt.uint32
ALU, ACT, AX = mybir.AluOpType, mybir.ActivationFunctionType, mybir.AxisListType


def build(nc, x, ctx, decay, first, gate, wi0, wi1, wo, out):
    weights = [w.rearrange("e (k p) m -> e p k m", p=P) for w in (wi0, wi1, wo)]
    x_in = x.rearrange("b (h p) c -> p (b h) c", p=P)
    v_in = ctx.rearrange("b (h p) c -> p (b h) c", p=P)
    out_rows = out.rearrange("b t c -> (b t) c")
    xn_rows = nc.dram_tensor("xn_rows", [NTOK, C], F32, kind="Internal").ap()
    table = nc.dram_tensor("table", [EX * NTOK, 2], I32, kind="Internal").ap()

    with ExitStack() as keep:
        def sb(name, shape, dt=F32, stack=keep):
            return stack.enter_context(nc.sbuf_tensor(name, shape, dt))

        def sem(name):
            return keep.enter_context(nc.semaphore(name))

        raw = sb("raw", [P, 3, NK, M])
        wh = [sb("wh0", [P, 3, NK, M], F32R), None]
        wl = [sb("wl0", [P, 3, NK, M], F32R), None]
        ident = sb("ident", [P, P])
        lists = sb("lists", [P, EX * JT + 1, 2], I32)
        totals = sb("totals", [P, EX])
        list_length = sb("list_length", [P, EX], I32)
        xg = sb("xg", [P, 2, C])
        acc = sb("acc", [P, CT, C])
        idx = sb("idx", [P, 2, CT], I32)
        tiles_over = sb("tiles_over", [P, 1], I32)
        over_expert = sb("over_expert", [P, OV], I32)
        over_column = sb("over_column", [P, OV], I32)
        over_iota = sb("over_iota", [P, OV])
        ones8 = sb("ones8", [P, EX])
        cnt_b = sb("cnt_b", [P, EX], I32); cnt_t = sb("cnt_t", [P, EX], I32)
        cnt_f = sb("cnt_f", [P, EX]); extra = sb("extra", [P, EX]); extra_sum = sb("extra_sum", [P, EX])
        past = sb("past", [P, OV, EX])
        past_experts = sb("past_experts", [P, OV]); past_tiles = sb("past_tiles", [P, OV])
        over_j = sb("over_j", [P, OV]); over_c = sb("over_c", [P, OV]); over_d = sb("over_d", [P, OV])

        phase_a = ExitStack()
        def sa(name, shape, dt=F32):
            return sb(name, shape, dt, phase_a)
        before = sa("before", [P, P], BF16)
        ones = sa("ones", [P, P], BF16)
        X = sa("X", [P, NT, C])
        K = sa("K", [P, GT, C])
        V = sa("V", [P, GT, C])
        decay_row = sa("decay_row", [P, NC, GW])
        f1 = sa("f1", [P, 2, GW])
        f2 = sa("f2", [P, 4, GW])
        vs = sa("vs", [P, 2, GW])
        g1 = sa("g1", [P, 2, GW])
        g2 = sa("g2", [P, 2, GW])
        st_a = sa("st_a", [P, 2, GW])
        st_b = sa("st_b", [P, 2, GW])
        Y = sa("Y", [P, NC, GW])
        XN = sa("XN", [P, GT, C])
        XNT = sa("XNT", [P, 2, NC, P])
        stat1 = sa("stat1", [P, NT, 6])
        mv1 = sa("mv1", [P, NT, 2])
        stat2 = sa("stat2", [P, GT, 6])
        mv2 = sa("mv2", [P, GT, 2])
        ve = sa("ve", [P, NT]); r0 = sa("r0", [P, NT]); na = sa("na", [P, NT]); nb = sa("nb", [P, NT])
        ncf = sa("ncf", [P, NT]); rs1 = sa("rs1", [P, NT]); nm1 = sa("nm1", [P, NT])
        ve2 = sa("ve2", [P, GT]); q0 = sa("q0", [P, GT]); qa = sa("qa", [P, GT]); qb = sa("qb", [P, GT])
        qc = sa("qc", [P, GT]); rs2 = sa("rs2", [P, GT]); nm2 = sa("nm2", [P, GT]); lnv = sa("lnv", [P, NT]); lnv2 = sa("lnv2", [P, GT])
        td = sa("td", [P, NC]); tf = sa("tf", [P, NC]); etd = sa("etd", [P, NC]); dd = sa("dd", [P, NC])
        ub1 = sa("ub1", [P, NC]); ub2 = sa("ub2", [P, NC])
        gk = sa("gk", [P, NC, EX])
        iota8 = sa("iota8", [P, EX])
        tok = sa("tok", [P, NT], I32)
        m8 = sa("m8", [P, GT, 8]); i8 = sa("i8", [P, GT, 8], U32)
        idxf = sa("idxf", [P, GT, 2]); dlt = sa("dlt", [P, GT]); e2 = sa("e2", [P, GT])
        e2p = sa("e2p", [P, GT])
        oh = sa("oh", [P, GT, 2, EX]); ohr = sa("ohr", [P, GT, 2, EX])
        msk = sa("msk", [P, GT, EX], BF16)
        cum = sa("cum", [P, EX], BF16)
        cum_add = sa("cum_add", [P, EX])
        place = sa("place", [P, GT, 2], I32); place_p = sa("place_p", [P, GT, 2], I32)
        place_j = sa("place_j", [P, GT, 2], I32)
        rows = [sa(f"rows{i}", [P, GT, 2], I32) for i in range(2)]
        recs = [sa(f"recs{i}", [P, GT, 2, 2], I32) for i in range(2)]
        blank = sa("blank", [P, P, 2], I32)
        phase_a.close()

        phase_b = ExitStack()
        def sbb(name, shape, dt=F32):
            return sb(name, shape, dt, phase_b)
        wh[1] = sbb("wh1", [P, 3, NK, M], F32R)
        wl[1] = sbb("wl1", [P, 3, NK, M], F32R)
        xth = [sbb(f"xth{i}", [P, NK, CAP], F32R) for i in range(2)]
        xtl = [sbb(f"xtl{i}", [P, NK, CAP], F32R) for i in range(2)]
        hth = sbb("hth", [P, NK, CAP], F32R)
        htl = sbb("htl", [P, NK, CAP], F32R)
        sl = sbb("sl", [P, 2, (CT - FT) * P])
        hm = sbb("hm", [P, 2, (CT - FT) * P])
        phase_b.close()

        phase_c = ExitStack()
        def sc(name, shape, dt=F32):
            return sb(name, shape, dt, phase_c)
        o_idx = sc("o_idx", [P, 2], I32)
        o_x = sc("o_x", [P, C]); o_acc = sc("o_acc", [P, C]); o_xt = sc("o_xt", [P, NK, P])
        o_s = sc("o_s", [P, M]); o_h = sc("o_h", [P, M]); o_ht = sc("o_ht", [P, NK, P]); o_r = sc("o_r", [P, C])
        phase_c.close()

        bank = [keep.enter_context(nc.psum_tensor(f"bank{i}", [P, 512], F32)) for i in range(8)]
        logits, ranks = ([bank[i][:, at:at + GT * EX].rearrange("p (j e) -> p j e", e=EX) for i in (6, 7)]
                         for at in (0, 64))

        x_loaded = [sem(f"x_loaded{g}") for g in range(NG)]
        small_loaded = sem("small_loaded")
        v_loaded = sem("v_loaded")
        blank_made = sem("blank_made"); table_blank = sem("table_blank")
        const_made = sem("const_made"); ident_made = sem("ident_made")
        decay_exp = sem("decay_exp"); dve_prologue = sem("dve_prologue")
        ln1 = sem("ln1"); ln1_act = sem("ln1_act"); ln1_stat = sem("ln1_stat"); ln1_sum = sem("ln1_sum")
        k_ready = sem("k_ready")
        k_turned = sem("k_turned")
        v_turned = sem("v_turned")
        f2_made = sem("f2_made")
        vs_made = sem("vs_made")
        b_scanned = sem("b_scanned")
        g1_made = sem("g1_made")
        a_scanned = sem("a_scanned")
        den_made = sem("den_made")
        g2_made = sem("g2_made")
        first_made = sem("first_made")
        num_made = sem("num_made")
        y_made = sem("y_made")
        ln_made = sem("ln_made"); rden_made = sem("rden_made")
        y_turned = sem("y_turned")
        x1_made = sem("x1_made")
        x1_stored = sem("x1_stored")
        xn_stored = [sem(f"xn_stored{j}") for j in range(GT)]
        xn_free = sem("xn_free")
        ln2 = sem("ln2"); ln2_act = sem("ln2_act")
        stat2_made = sem("stat2_made"); mv2_made = sem("mv2_made")
        xn_made = sem("xn_made")
        xn_turned = sem("xn_turned")
        xnt_made = sem("xnt_made")
        gated = sem("gated")
        route = sem("route")
        mask_made = sem("mask_made"); delta_made = sem("delta_made"); e2_made = sem("e2_made")
        ranked = sem("ranked")
        ranks_read = sem("ranks_read")
        rows_made = sem("rows_made")
        rec_stored = sem("rec_stored")
        row_init = sem("row_init")
        totals_made = sem("totals_made")
        raw_loaded = [sem(f"raw_loaded{m}") for m in range(3)]
        wh_made = sem("wh_made"); wl_made = sem("wl_made")
        lists_loaded = sem("lists_loaded")
        phase_a_done = sem("phase_a_done")
        b_cleared = sem("b_cleared")
        idx_made = sem("idx_made")
        xg_loaded = [sem(f"xg_loaded{i}") for i in range(2)]
        xg_turned = sem("xg_turned")
        xh_made = sem("xh_made")
        xl_made = sem("xl_made")
        h0_done = sem("h0_done"); h1_done = sem("h1_done")
        silu_made = sem("silu_made")
        hm_made = sem("hm_made")
        hh_made = sem("hh_made"); hl_made = sem("hl_made")
        out_done = sem("out_done")
        fin_made = sem("fin_made")
        acc_loaded = [sem(f"acc_loaded{j}") for j in range(CT)]
        acc_stored = [sem(f"acc_stored{j}") for j in range(CT)]
        over_made = sem("over_made"); over_ready = sem("over_ready")
        o_w = sem("o_w"); o_copied = sem("o_copied"); o_xin = sem("o_xin"); o_ain = sem("o_ain")
        o_xturn = sem("o_xturn"); o_xtm = sem("o_xtm"); o_h01 = sem("o_h01"); o_sm = sem("o_sm")
        o_hm = sem("o_hm"); o_hturn = sem("o_hturn"); o_htm = sem("o_htm"); o_out = sem("o_out")
        o_fin = sem("o_fin"); o_sto = sem("o_sto")

        waits_ended = sem("waits_ended")
        LN1_STEPS = 4
        ROUTE_STEPS = 14

        def apart(engine):
            engine.sem_inc(waits_ended, 1)

        block = keep.enter_context(nc.Block())

        @block.sync
        def _(sp):
            for g in range(NG):
                sp.dma_start(X[:, g * GT:(g + 1) * GT, :], x_in[:, g * GT:(g + 1) * GT, :]).then_inc(x_loaded[g], 16)
                if g == 0:
                    sp.dma_start(td[:, :], decay).then_inc(small_loaded, 16)
                    sp.dma_start(tf[:, :], first).then_inc(small_loaded, 16)
                    sp.dma_start(gk[:, :, :], gate).then_inc(small_loaded, 16)
                if g == 1:
                    sp.dma_start(V[:, :, :], v_in[:, 0:GT, :]).then_inc(v_loaded, 16)
            sp.wait_ge(blank_made, 2)
            sp.dma_start(table.rearrange("(p n) w -> p n w", p=P), blank[:, :, :]).then_inc(table_blank, 16)
            for m in range(3):
                sp.dma_start(raw[:, m, :, :], weights[m][0]).then_inc(raw_loaded[m], 16)

            def store(b):
                for j in range(GT):
                    t = b * GT + j
                    sp.wait_ge(x1_made, t + 5)
                    sp.dma_start(out_rows[bass.ds(t * P, P), :], X[:, t, :]).then_inc(x1_stored, 16)
                for j in range(GT):
                    t = b * GT + j
                    sp.wait_ge(xn_made, t + 1)
                    sp.dma_start(xn_rows[bass.ds(t * P, P), :], XN[:, j, :]).then_inc(xn_stored[j], 16)
                for j in range(GT):
                    sp.wait_ge(xn_stored[j], b * 16 + 16)
                sp.sem_inc(xn_free, 1)

            sp.wait_ge(v_turned, NC)
            sp.dma_start(V[:, :, :], v_in[:, GT:2 * GT, :]).then_inc(v_loaded, 16)
            with sp.Fori(1, NG - 1) as s:
                sp.wait_ge(v_turned, (s + 1) * NC)
                sp.dma_start(V[:, :, :], v_in[:, bass.ds((s + 1) * GT, GT), :]).then_inc(v_loaded, 16)
                store(s - 1)
            store(NG - 2)
            store(NG - 1)
            sp.wait_ge(rec_stored, 16 * 2 * GT * (NG + 1))
            sp.wait_ge(x1_stored, 16 * NT)
            sp.sem_inc(phase_a_done, 1)
            sp.dma_start(lists[:, 0:EX * JT, :], table.rearrange("(p n) w -> p n w", p=P)).then_inc(lists_loaded, 16)
            sp.wait_ge(xh_made, FT)
            with sp.Fori(1, EX) as e:
                for m in range(3):
                    sp.wait_ge(wl_made, (e - 1) * 3 * NK + NK * (m + 1))
                    sp.dma_start(raw[:, m, :, :], weights[m][e]).then_inc(raw_loaded[m], 16)
            sp.wait_ge(over_ready, 1)
            sp.wait_ge(fin_made, EX * CT + 2)
            over = sp.value_load(tiles_over[0:1, 0:1], min_val=0, max_val=OV)
            with sp.If(over > 0):
                with sp.Fori(0, OV) as k:
                    sp.wait_ge(o_fin, k + 1)
                    e = sp.value_load(over_expert[0:1, bass.ds(k, 1)], min_val=0, max_val=EX - 1)
                    for m in range(3):
                        sp.dma_start(raw[:, m, :, :], weights[m][e]).then_inc(o_w, 16)

        @block.gpsimd
        def _(pool):
            for s_, n in ((f2_made, 2), (vs_made, 2), (b_scanned, 2), (den_made, 2),
                          (first_made, 2), (y_made, 4), (y_turned, 1), (x1_made, 4), (xnt_made, 2), (xn_free, 1),
                          (gated, 2), (ranks_read, 1), (xg_turned, 2), (xl_made, 2), (silu_made, 2),
                          (hm_made, 2), (out_done, 1), (fin_made, 2), (o_fin, 1)):
                pool.sem_inc(s_, n)
            pool.memset(ident[:, :], 0.0).then_inc(ident_made, 1)
            pool.wait_ge(ident_made, 1)
            pool.affine_select(out=ident[:, :], in_=ident[:, :], compare_op=ALU.not_equal, fill=1.0, base=0,
                               pattern=[[-1, P]], channel_multiplier=1).then_inc(ident_made, 1)
            pool.memset(before[:, :], 1.0).then_inc(const_made, 1)
            pool.memset(ones[:, :], 1.0)
            pool.memset(blank[:, :, 0], OOB).then_inc(blank_made, 1)
            pool.memset(blank[:, :, 1], 0).then_inc(blank_made, 1)
            pool.memset(lists[:, EX * JT, 0:1], OOB)
            pool.memset(lists[:, EX * JT, 1:2], 0)
            pool.memset(rows[0][:, :, :], EX * NTOK).then_inc(row_init, 1)
            pool.memset(recs[0][:, :, :, :], 0).then_inc(row_init, 1)
            pool.iota(cum[:, :], [[NTOK // P, EX]], base=0, channel_multiplier=0,
                      allow_small_or_imprecise_dtypes=True)
            pool.memset(xg[:, :, :], 0.0).then_inc(b_cleared, 1)
            pool.memset(acc[:, :, :], 0.0).then_inc(b_cleared, 1)
            pool.iota(tok[:, :], [[P, NT]], base=0, channel_multiplier=1)
            pool.iota(over_iota[:, :], [[1, OV]], base=0, channel_multiplier=0, allow_small_or_imprecise_dtypes=True)
            pool.memset(ones8[:, :], 1.0)
            pool.iota(iota8[:, :], [[1, EX]], base=0, channel_multiplier=0, allow_small_or_imprecise_dtypes=True)
            pool.wait_ge(const_made, 1)
            pool.affine_select(out=before[:, :], in_=before[:, :], compare_op=ALU.is_gt, fill=0.0, base=0,
                               pattern=[[1, P]], channel_multiplier=-1).then_inc(const_made, 1)
            pool.wait_ge(table_blank, 16)

            def store_entries(n, last=0):
                row, rec = rows[last], recs[last]
                for i in n:
                    j, c = i // 2, i % 2
                    pool.indirect_dma_start(table, bass.IndirectOffsetOnAxis(ap=row[:, j, c:c + 1], axis=0),
                                            rec[:, j, c, :], None, bounds_check=last_entry,
                                            oob_is_err=False).then_inc(rec_stored, 16)

            last_entry, last_token = pool.to_reg(EX * NTOK - 1), pool.to_reg(NTOK - 1)

            def first_steps(s, c):
                if c == 0:
                    pool.wait_ge(y_turned, s * GT + 1)
                apart(pool)
                pool.tensor_copy(Y[:, c, 0:GW:T], vs[:, c % 2, 0:GW:T]).then_inc(first_made, 1)

            def unit(s, c, between=range(0)):
                un = s * NC + c
                vb, fb, gb = vs[:, c % 2, :], f2[:, c, :], g2[:, c % 2, :]
                pool.wait_ge(vs_made, un + 3)
                pool.wait_ge(f2_made, un + 3)
                pool.wait_ge(y_made, un + 3)
                pool.tensor_tensor(gb, fb, vb, ALU.mult).then_inc(g2_made, 1)
                store_entries(between)
                pool.wait_ge(b_scanned, un + 3)
                fv = fb.rearrange("p (b t) -> p b t", t=T)[:, :, 1:T]
                sv = st_b[:, c % 2, :].rearrange("p (b t) -> p b t", t=T)[:, :, 1:T]
                pool.wait_ge(g2_made, un + 1)
                pool.tensor_tensor(fv, fv, sv, ALU.add).then_inc(den_made, 1)

            def group(s, stores, more):
                if stores:
                    pool.wait_ge(row_init, 2)
                    pool.wait_ge(rows_made, s)
                    apart(pool)
                    store_entries(range(0, 3))
                first_steps(s, 0)
                first_steps(s, 1)
                if stores:
                    store_entries(range(3, 5))
                unit(s, 2, range(5, 2 * GT) if stores else range(0))
                first_steps(s, 2)
                unit(s, 3)
                first_steps(s, 3)
                if more:
                    unit(s + 1, 0)
                    unit(s + 1, 1)

            unit(0, 0)
            unit(0, 1)
            group(0, False, True)
            with pool.Fori(1, NG - 1) as s:
                group(s, True, True)
            group(NG - 1, True, False)
            for k, n, last in ((NG, range(2 * GT), 0), (NG + 1, range(GT), 1), (NG + 2, range(GT, 2 * GT), 1)):
                pool.wait_ge(rows_made, k)
                apart(pool)
                store_entries(n, last)

            pool.wait_ge(b_cleared, 2)
            pool.wait_ge(lists_loaded, 16)
            lists_e = lists[:, 0:EX * JT, :].rearrange("p (e j) w -> p e j w", e=EX)

            def gather_x(p, i):
                r, j = i // CT, i % CT
                if j == 0:
                    pool.tensor_copy(idx[:, r, :], lists_e[:, p * 2 + r, 0:CT, 0]).then_inc(idx_made, 1)
                    pool.wait_ge(idx_made, p * 2 + r + 1)
                pool.wait_ge(xg_turned, p * 2 * CT + i + 1)
                apart(pool)
                pool.indirect_dma_start(xg[:, i % 2, :], None, xn_rows,
                                        bass.IndirectOffsetOnAxis(ap=idx[:, r, j:j + 1], axis=0),
                                        bounds_check=last_token, oob_is_err=False).then_inc(xg_loaded[i % 2], 16)

            def expert(p, r, last):
                e = p * 2 + r
                nxt = [(p, CT + j) if r == 0 else (p + 1, j) for j in range(CT)]
                if not last:
                    gather_x(*nxt[0])
                    gather_x(*nxt[1])
                apart(pool)
                for j in range(CT):
                    pool.indirect_dma_start(acc[:, j, :], None, out_rows,
                                            bass.IndirectOffsetOnAxis(ap=idx[:, r, j:j + 1], axis=0),
                                            bounds_check=last_token, oob_is_err=False).then_inc(acc_loaded[j], 16)
                if not last:
                    gather_x(*nxt[2])
                    gather_x(*nxt[3])
                for j in range(CT):
                    pool.wait_ge(fin_made, e * CT + j + 3)
                    apart(pool)
                    pool.indirect_dma_start(out_rows, bass.IndirectOffsetOnAxis(ap=idx[:, r, j:j + 1], axis=0),
                                            acc[:, j, :], None, bounds_check=last_token,
                                            oob_is_err=False).then_inc(acc_stored[j], 16)
                if not last:
                    gather_x(*nxt[4])
                for j in range(CT):
                    pool.wait_ge(acc_stored[j], (e + 1) * 16)

            for j in range(CT):
                gather_x(0, j)
            with pool.Fori(0, EX // 2 - 1) as p:
                expert(p, 0, False)
                expert(p, 1, False)
            expert(EX // 2 - 1, 0, False)
            expert(EX // 2 - 1, 1, True)

            pool.wait_ge(over_ready, 1)
            pool.wait_ge(fin_made, EX * CT + 2)
            over = pool.value_load(tiles_over[0:1, 0:1], min_val=0, max_val=OV)
            with pool.If(over > 0):
                with pool.Fori(0, OV) as k:
                    pool.wait_ge(o_fin, k + 1)
                    col = pool.value_load(over_column[0:1, bass.ds(k, 1)], min_val=0, max_val=EX * JT)
                    pool.tensor_copy(o_idx[:, :], lists[:, col, :]).then_inc(o_copied, 1)
                    pool.memset(o_x[:, :], 0.0).then_inc(o_copied, 1)
                    pool.memset(o_acc[:, :], 0.0).then_inc(o_copied, 1)
                    pool.wait_ge(o_copied, k * 3 + 3)
                    apart(pool)
                    for dst, src, s_ in ((o_x, xn_rows, o_xin), (o_acc, out_rows, o_ain)):
                        pool.indirect_dma_start(dst[:, :], None, src,
                                                bass.IndirectOffsetOnAxis(ap=o_idx[:, 0:1], axis=0),
                                                bounds_check=last_token, oob_is_err=False).then_inc(s_, 16)
                    pool.wait_ge(o_fin, k + 2)
                    apart(pool)
                    pool.indirect_dma_start(out_rows, bass.IndirectOffsetOnAxis(ap=o_idx[:, 0:1], axis=0),
                                            o_r[:, :], None, bounds_check=last_token,
                                            oob_is_err=False).then_inc(o_sto, 16)
                    pool.wait_ge(o_sto, k * 16 + 16)

        @block.scalar
        def _(act):
            act.add_instruction(mybir.InstLoadActFuncSet(name=nc.get_next_instruction_name(),
                                                         act_func_set_id=EXP_LN_SET))
            act.wait_ge(small_loaded, 48)
            act.activation(etd[:, :], td[:, :], ACT.Exp).then_inc(decay_exp, 1)
            act.wait_ge(decay_exp, 1)
            act.activation(dd[:, :], etd[:, :], ACT.Exp, scale=-1.0).then_inc(decay_exp, 1)

            def first_inv_sqrt(start, log, v, n):
                act.wait_ge(ln1, n * (LN1_STEPS + 2) + 1)
                act.activation(log, v, ACT.Ln).then_inc(ln1_act, 1)
                act.wait_ge(ln1_act, n * 2 + 1)
                act.activation(start, log, ACT.Exp, scale=-0.5).then_inc(ln1_act, 1)

            def exponentials(s, c):
                un = s * NC + c
                act.wait_ge(k_turned, un + 1)
                act.wait_ge(b_scanned, un + 1)
                act.activation(f1[:, c % 2, :], bank[c % 2][:, :], ACT.Exp, bias=ub1[:, c:c + 1])
                act.wait_ge(y_made, un + 1)
                act.activation(f2[:, c, :], bank[c % 2][:, :], ACT.Exp, bias=ub2[:, c:c + 1]).then_inc(f2_made, 1)
                act.wait_ge(v_turned, un + 1)
                act.wait_ge(first_made, un + 1)
                act.activation(vs[:, c % 2, :], bank[2 + c % 2][:, :], ACT.Copy).then_inc(vs_made, 1)

            def inverse(s, c):
                un = s * NC + c
                fv = f2[:, c, :].rearrange("p (b t) -> p b t", t=T)[:, :, 1:T]
                act.wait_ge(den_made, un + 3)
                act.activation(fv, fv, ACT.Ln).then_inc(ln_made, 1)
                act.wait_ge(ln_made, un + 1)
                act.activation(fv, fv, ACT.Exp, scale=-1.0).then_inc(rden_made, 1)

            def normalise(g):
                for j in range(GT):
                    t = g * GT + j
                    act.activation(K[:, j, :], X[:, t, :], ACT.Identity, bias=nm1[:, bass.ds(t, 1)],
                                   scale=rs1[:, bass.ds(t, 1)]).then_inc(k_ready, 1)

            def normalised(b):
                act.wait_ge(xn_free, b + 1)
                act.wait_ge(ln2, (b + 1) * (LN1_STEPS + 2))
                for j in range(GT):
                    act.activation(XN[:, j, :], X[:, b * GT + j, :], ACT.Identity, bias=nm2[:, j:j + 1],
                                   scale=rs2[:, j:j + 1]).then_inc(xn_made, 1)

            def turned_norm(b, tiles):
                for j in tiles:
                    t = b * GT + j
                    act.wait_ge(xn_turned, t + 1)
                    act.wait_ge(gated, t + 1)
                    act.activation(XNT[:, j % 2, :, :], bank[4 + j % 2].rearrange("p (k n) -> p k n", n=P),
                                   ACT.Copy).then_inc(xnt_made, 1)

            def ln2_start(b):
                act.wait_ge(ln2, b * (LN1_STEPS + 2) + 1)
                act.activation(lnv2[:, :], ve2[:, :], ACT.Ln).then_inc(ln2_act, 1)
                act.wait_ge(ln2_act, b * 2 + 1)
                act.activation(q0[:, :], lnv2[:, :], ACT.Exp, scale=-0.5).then_inc(ln2_act, 1)

            def weights(k, w=slice(0, GT)):
                act.wait_ge(delta_made, k + 1)
                act.activation(e2[:, w], dlt[:, w], ACT.Exp).then_inc(e2_made, 1)

            def group(s, back, more):
                b = s - 1
                inverse(s, 0)
                inverse(s, 1)
                exponentials(s, 2)
                if not back:
                    act.wait_ge(ln1, 2 * (LN1_STEPS + 2))
                if more:
                    act.wait_ge(k_turned, (s + 1) * NC)
                    normalise(s + 1)
                if back:
                    ln2_start(b)
                exponentials(s, 3)
                if back:
                    normalised(b)
                if back:
                    turned_norm(b, (0,))
                inverse(s, 2)
                if back:
                    turned_norm(b, (1,))
                if more:
                    exponentials(s + 1, 0)
                inverse(s, 3)
                if back:
                    turned_norm(b, (2,))
                if more:
                    exponentials(s + 1, 1)
                if back:
                    turned_norm(b, (3,))
                if not more:
                    ln2_start(s)
                    normalised(s)
                if back:
                    weights(b)

            first_inv_sqrt(r0[:, 0:GT], lnv[:, 0:GT], ve[:, 0:GT], 0)
            act.wait_ge(ln1, LN1_STEPS + 2)
            normalise(0)
            exponentials(0, 0)
            exponentials(0, 1)
            first_inv_sqrt(r0[:, GT:NT], lnv[:, GT:NT], ve[:, GT:NT], 1)
            group(0, False, True)
            with act.Fori(1, NG - 1) as s:
                group(s, True, True)
            group(NG - 1, True, False)
            turned_norm(NG - 1, range(GT))
            weights(NG - 1, slice(0, GT // 2))
            weights(NG, slice(GT // 2, GT))
            for n in range(3 * NK):
                if n % NK == 0:
                    act.wait_ge(raw_loaded[n // NK], 16)
                act.activation(wh[0][:, n // NK, n % NK, :], raw[:, n // NK, n % NK, :], ACT.Copy).then_inc(wh_made, 1)
            act.wait_ge(e2_made, NG + 1)
            act.sem_inc(phase_a_done, 1)

            act.wait_ge(phase_a_done, 4)

            def x_high(p, i):
                r, j, tt = i // CT, i % CT, p * 2 * CT + i
                act.wait_ge(xg_turned, tt + 3)
                act.activation(xth[r][:, :, j * P:(j + 1) * P], bank[6 + i % 2].rearrange("p (k n) -> p k n", n=P),
                               ACT.Copy).then_inc(xh_made, 1)

            def w_high(p, r, n):
                e, m = p * 2 + r, n // NK
                if n == 0:
                    act.wait_ge(out_done, e * CT + 1)
                if n % NK == 0:
                    act.wait_ge(raw_loaded[m], (e + 2) * 16)
                act.activation(wh[1 - r][:, m, n % NK, :], raw[:, m, n % NK, :], ACT.Copy).then_inc(wh_made, 1)

            def h_high(p, r, l):
                hb = (p * 2 + r) * 2 * NK + l
                act.wait_ge(hm_made, hb + 3)
                w = PARTS[l // NK]
                act.activation(hth[:, l % NK, w], hm[:, l % 2, 0:w.stop - w.start], ACT.Copy).then_inc(hh_made, 1)

            def silu(p, r, l):
                hb = (p * 2 + r) * 2 * NK + l
                act.wait_ge(h0_done, hb + 1)
                act.wait_ge(hm_made, hb + 1)
                n = PARTS[l // NK].stop - PARTS[l // NK].start
                act.activation(sl[:, l % 2, 0:n], bank[l % 2][:, 0:n], ACT.Silu).then_inc(silu_made, 1)

            def expert(p, r, last):
                nxt = [(p, CT + j) if r == 0 else (p + 1, j) for j in range(CT)]
                for l in range(2 * NK):
                    if l > 0:
                        h_high(p, r, l - 1)
                    silu(p, r, l)
                    if l in (1, 2, 3):
                        x_high(p, r * CT + l + 1)
                    if l in (6, 7) and not last:
                        x_high(*nxt[l - 6])
                    if l >= 2 and not last:
                        w_high(p, r, l - 2)
                h_high(p, r, 2 * NK - 1)
                if not last:
                    for n in range(2 * NK - 2, 3 * NK):
                        w_high(p, r, n)

            for j in range(FT):
                x_high(0, j)
            with act.Fori(0, EX // 2 - 1) as p:
                expert(p, 0, False)
                expert(p, 1, False)
            expert(EX // 2 - 1, 0, False)
            expert(EX // 2 - 1, 1, True)

            act.wait_ge(over_ready, 1)
            act.wait_ge(fin_made, EX * CT + 2)
            over = act.value_load(tiles_over[0:1, 0:1], min_val=0, max_val=OV)
            with act.If(over > 0):
                with act.Fori(0, OV) as k:
                    act.wait_ge(o_xturn, k + 1)
                    act.activation(o_xt[:, :, :], bank[6].rearrange("p (k n) -> p k n", n=P), ACT.Copy).then_inc(o_xtm, 1)
                    act.wait_ge(o_h01, k + 1)
                    act.activation(o_s[:, :], bank[0][:, :], ACT.Silu).then_inc(o_sm, 1)
                    act.wait_ge(o_hturn, k + 1)
                    act.activation(o_ht[:, :, :], bank[7].rearrange("p (k n) -> p k n", n=P), ACT.Copy).then_inc(o_htm, 1)

        @block.vector
        def _(dve):
            def inv_sqrt(v, start, a, b, c, r, sem_, base, n):
                steps = (lambda: dve.tensor_tensor(a, start, start, ALU.mult),
                         lambda: dve.tensor_tensor(b, a, v, ALU.mult),
                         lambda: dve.tensor_scalar(c, b, -0.5, 1.5, ALU.mult, ALU.add),
                         lambda: dve.tensor_tensor(r, c, start, ALU.mult))
                for i in range(len(steps)):
                    steps[i]().then_inc(sem_, 1)
                    dve.wait_ge(sem_, base + i + 1)

            dve.memset(decay_row[:, :, :], 1.0).then_inc(dve_prologue, 1)
            dve.wait_ge(small_loaded, 48)
            dve.tensor_scalar(ub1[:, :], tf[:, :], 0.0, -1.0, ALU.max, ALU.mult)
            dve.tensor_scalar(ub2[:, :], tf[:, :], 0.0, None, ALU.min)

            def ln1_stats(g):
                dve.wait_ge(x_loaded[g], 16)
                for t in range(g * GT, (g + 1) * GT):
                    dve.bn_stats(stat1[:, t, :], X[:, t, :]).then_inc(ln1_stat, 1)

            def ln1_sums(t0, t1, n):
                for t in range(t0, t1):
                    dve.wait_ge(ln1_stat, t + 1)
                    apart(dve)
                    ins = dve.bn_aggr(mv1[:, t, :], stat1[:, t, :])
                ins.then_inc(ln1_sum, 1)
                dve.wait_ge(ln1_sum, n + 1)
                dve.tensor_scalar(ve[:, t0:t1], mv1[:, t0:t1, 1], EPS, None, ALU.add).then_inc(ln1, 1)

            def ln1_finish(t0, t1, n):
                w = slice(t0, t1)
                dve.wait_ge(ln1_act, 2 * n + 2)
                dve.wait_ge(ln1, n * (LN1_STEPS + 2) + 1)
                inv_sqrt(ve[:, w], r0[:, w], na[:, w], nb[:, w], ncf[:, w], rs1[:, w], ln1,
                         n * (LN1_STEPS + 2) + 1, NT)
                dve.scalar_tensor_tensor(nm1[:, w], mv1[:, w, 0], -1.0, rs1[:, w], ALU.mult, ALU.mult).then_inc(ln1, 1)

            ln1_stats(0)
            ln1_sums(0, GT, 0)
            ln1_finish(0, GT, 0)
            dve.wait_ge(decay_exp, 2)
            dve.wait_ge(dve_prologue, 1)
            for c in range(NC):
                last = dve.tensor_scalar(decay_row[:, c, :], decay_row[:, c, :], dd[:, c:c + 1], None, ALU.mult)
            last.then_inc(dve_prologue, 1)
            dve.wait_ge(dve_prologue, 2)
            dve.memset(decay_row[:, :, T:T + 1], 0.0).then_inc(dve_prologue, 1)
            dve.wait_ge(dve_prologue, 3)
            dve.sem_inc(rows_made, 1)
            for g in range(1, NG):
                ln1_stats(g)

            def finish_y(s, c):
                un = s * NC + c
                yv, nv, rv = (z.rearrange("p (b t) -> p b t", t=T)[:, :, 1:T]
                              for z in (Y[:, c, :], g2[:, c % 2, :], f2[:, c, :]))
                dve.wait_ge(num_made, un + 1)
                dve.wait_ge(rden_made, un + 1)
                if c == 0:
                    dve.wait_ge(y_turned, s * GT + 1)
                dve.tensor_tensor(yv, nv, rv, ALU.mult).then_inc(y_made, 1)

            def scans(s, c):
                un, q = s * NC + c, c % 2
                dve.wait_ge(f2_made, un + 3)
                dve.wait_ge(vs_made, un + 3)
                dve.tensor_tensor(g1[:, q, :], f1[:, q, :], vs[:, q, :], ALU.mult).then_inc(g1_made, 1)
                dve.wait_ge(den_made, un + 1)
                dve.tensor_tensor_scan(st_b[:, q, 1:GW], decay_row[:, c, 0:GW - 1], f1[:, q, 0:GW - 1], 0.0,
                                       ALU.mult, ALU.add).then_inc(b_scanned, 1)
                dve.wait_ge(g1_made, un + 1)
                dve.tensor_tensor_scan(st_a[:, q, 1:GW], decay_row[:, c, 0:GW - 1], g1[:, q, 0:GW - 1], 0.0,
                                       ALU.mult, ALU.add).then_inc(a_scanned, 1)

            def numerator(s, c):
                un, q = s * NC + c, c % 2
                gv, av = (z.rearrange("p (b t) -> p b t", t=T)[:, :, 1:T] for z in (g2[:, q, :], st_a[:, q, :]))
                dve.wait_ge(g2_made, un + 1)
                dve.wait_ge(a_scanned, un + 1)
                dve.tensor_tensor(gv, gv, av, ALU.add).then_inc(num_made, 1)

            def w_low(h, l, r):
                return dve.tensor_tensor(l, r, h.bitcast(F32), ALU.subtract)

            def routing(g, tiles=range(GT), k=None, last=0, at=0):
                k = g if k is None else k
                row, rec, recf = rows[last], recs[last], recs[last].bitcast(F32)
                w, nt = slice(tiles.start, tiles.stop), len(tiles)

                def done(n):
                    dve.wait_ge(route, k * ROUTE_STEPS + n)

                dve.wait_ge(gated, g * GT + tiles.stop + 2)
                if not last:
                    dve.wait_ge(rec_stored, (g + 1) * 16 * 2 * GT)
                apart(dve)
                for j in tiles:
                    ins = dve.max(m8[:, j, :], logits[at][:, j, :])
                ins.then_inc(route, 1)
                done(1)
                apart(dve)
                for j in tiles:
                    ins = dve.max_index(i8[:, j, :], m8[:, j, :], logits[at][:, j, :])
                ins.then_inc(route, 1)
                dve.tensor_tensor(dlt[:, w], m8[:, w, 1], m8[:, w, 0], ALU.subtract).then_inc(delta_made, 1)
                done(2)
                dve.tensor_copy(idxf[:, w, :], i8[:, w, 0:2]).then_inc(route, 1)
                dve.tensor_copy(rec[:, w, :, 0], tok[:, bass.ds(g * GT + tiles.start, nt)][:, :, None]
                                .to_broadcast([P, nt, 2])).then_inc(route, 1)
                done(3)
                dve.tensor_tensor(oh[:, w, :, :], iota8[:, None, None, :].to_broadcast([P, nt, 2, EX]),
                                  idxf[:, w, :, None].to_broadcast([P, nt, 2, EX]),
                                  ALU.is_equal).then_inc(route, 1)
                done(5)
                dve.tensor_tensor(msk[:, w, :], oh[:, w, 0, :], oh[:, w, 1, :], ALU.add).then_inc(mask_made, 1)
                dve.wait_ge(e2_made, k + 1)
                dve.tensor_scalar(e2p[:, w], e2[:, w], 1.0, None, ALU.add).then_inc(route, 1)
                dve.wait_ge(mask_made, k + 1)
                dve.tensor_reduce(cum_add[:, :], msk.rearrange("p j e -> p e j"), AX.X, ALU.add).then_inc(route, 1)
                done(6)
                dve.reciprocal(recf[:, w, 0, 1], e2p[:, w]).then_inc(route, 1)
                dve.wait_ge(ranked, k + 1)
                dve.tensor_tensor(ohr[:, w, :, :], oh[:, w, :, :],
                                  ranks[at][:, w, None, :].to_broadcast([P, nt, 2, EX]),
                                  ALU.mult).then_inc(route, 1)
                done(8)
                dve.tensor_tensor(recf[:, w, 1, 1], recf[:, w, 0, 1], e2[:, w], ALU.mult).then_inc(route, 1)
                done(9)
                with nc.allow_low_precision(reason="whole numbers below 2 ** 14"):
                    dve.tensor_reduce(place[:, w, :], ohr[:, w, :, :], AX.X, ALU.add).then_inc(route, 1)
                if tiles.stop == GT:
                    dve.tensor_tensor(cum[:, :], cum[:, :], cum_add[:, :], ALU.add).then_inc(ranks_read, 1)
                done(11)
                dve.tensor_scalar(place_p[:, w, :], place[:, w, :], P - 1, (EX * JT).bit_length() - 1,
                                  ALU.bitwise_and, ALU.logical_shift_left).then_inc(route, 1)
                dve.tensor_scalar(place_j[:, w, :], place[:, w, :], P.bit_length() - 1, None,
                                  ALU.logical_shift_right).then_inc(route, 1)
                done(13)
                dve.tensor_tensor(row[:, w, :], place_p[:, w, :], place_j[:, w, :],
                                  ALU.bitwise_or).then_inc(route, 1)
                done(ROUTE_STEPS)
                dve.sem_inc(rows_made, 1)

            dve.wait_ge(const_made, 2)

            def residual(b, tiles, first_bank=4):
                for j in tiles:
                    t = b * GT + j
                    dve.wait_ge(y_turned, t + 2)
                    dve.tensor_tensor(X[:, t, :], X[:, t, :], bank[first_bank + j][:, :], ALU.add).then_inc(x1_made, 1)
                    if j % 2:
                        for i in (j - 1, j):
                            dve.wait_ge(x1_made, b * GT + i + 5)
                            apart(dve)
                            dve.bn_stats(stat2[:, i, :], X[:, b * GT + i, :]).then_inc(stat2_made, 1)

            def ln2_sums(b):
                for j in range(GT):
                    dve.wait_ge(stat2_made, b * GT + j + 1)
                    apart(dve)
                    ins = dve.bn_aggr(mv2[:, j, :], stat2[:, j, :])
                ins.then_inc(mv2_made, 1)
                dve.wait_ge(mv2_made, b + 1)
                dve.tensor_scalar(ve2[:, :], mv2[:, :, 1], EPS, None, ALU.add).then_inc(ln2, 1)

            def ln2_finish(b):
                dve.wait_ge(ln2_act, b * 2 + 2)
                dve.wait_ge(ln2, b * (LN1_STEPS + 2) + 1)
                inv_sqrt(ve2[:, :], q0[:, :], qa[:, :], qb[:, :], qc[:, :], rs2[:, :], ln2,
                         b * (LN1_STEPS + 2) + 1, GT)
                dve.scalar_tensor_tensor(nm2[:, :], mv2[:, :, 0], -1.0, rs2[:, :], ALU.mult, ALU.mult).then_inc(ln2, 1)

            def group(s, back, more):
                b = s - 1
                if back:
                    residual(b, (0, 1))
                finish_y(s, 0)
                numerator(s, 1)
                if back:
                    residual(b, (2, 3))
                    ln2_sums(b)
                finish_y(s, 1)
                if back:
                    ln2_finish(b)
                scans(s, 2)
                numerator(s, 2)
                scans(s, 3)
                finish_y(s, 2)
                numerator(s, 3)
                if more:
                    scans(s + 1, 0)
                finish_y(s, 3)
                if more:
                    numerator(s + 1, 0)
                    scans(s + 1, 1)
                else:
                    residual(s, range(GT), 0)
                    ln2_sums(s)
                    ln2_finish(s)
                if back:
                    routing(b)

            scans(0, 0)
            numerator(0, 0)
            scans(0, 1)
            ln1_sums(GT, NT, 1)
            ln1_finish(GT, NT, 1)
            group(0, False, True)
            with dve.Fori(1, NG - 1) as s:
                group(s, True, True)
            group(NG - 1, True, False)
            routing(NG - 1, range(0, GT // 2), NG - 1, 1, 1)
            routing(NG - 1, range(GT // 2, GT), NG, 1, 0)
            dve.wait_ge(rows_made, NG + 2)
            dve.wait_ge(totals_made, 1)
            dve.scalar_tensor_tensor(totals[:, :], iota8[:, :], -float(NTOK), bank[7][:, 128:128 + EX],
                                     ALU.mult, ALU.add).then_inc(over_made, 1)
            dve.wait_ge(over_made, 1)
            dve.sem_inc(phase_a_done, 1)
            for n in range(3 * NK):
                m, k = n // NK, n % NK
                dve.wait_ge(wh_made, n + 1)
                w_low(wh[0][:, m, k, :], wl[0][:, m, k, :], raw[:, m, k, :]).then_inc(wl_made, 1)

            n = [1]

            def step(ins):
                n[0] += 1
                ins.then_inc(over_made, 1)
                dve.wait_ge(over_made, n[0])

            step(dve.tensor_copy(list_length[:, :], totals[:, :]))
            step(dve.tensor_scalar(cnt_f[:, :], totals[:, :], float(P - 1), None, ALU.add))
            step(dve.tensor_copy(cnt_b[:, :], cnt_f[:, :]))
            step(dve.tensor_scalar(cnt_t[:, :], cnt_b[:, :], P.bit_length() - 1, None, ALU.logical_shift_right))
            step(dve.tensor_copy(cnt_f[:, :], cnt_t[:, :]))
            step(dve.tensor_scalar(extra[:, :], cnt_f[:, :], -float(CT), 0.0, ALU.add, ALU.max))
            step(dve.tensor_tensor_scan(extra_sum[:, :], ones8[:, :], extra[:, :], 0.0, ALU.mult, ALU.add))
            step(dve.tensor_copy(tiles_over[:, :], extra_sum[:, EX - 1:EX]))
            step(dve.tensor_tensor(past[:, :, :], over_iota[:, :, None].to_broadcast([P, OV, EX]),
                                   extra_sum[:, None, :].to_broadcast([P, OV, EX]), ALU.is_ge))
            step(dve.tensor_reduce(past_experts[:, :], past[:, :, :], AX.X, ALU.add))
            step(dve.tensor_tensor(past[:, :, :], past[:, :, :],
                                   extra[:, None, :].to_broadcast([P, OV, EX]), ALU.mult))
            step(dve.tensor_reduce(past_tiles[:, :], past[:, :, :], AX.X, ALU.add))
            step(dve.tensor_tensor(over_j[:, :], over_iota[:, :], past_tiles[:, :], ALU.subtract))
            step(dve.scalar_tensor_tensor(over_c[:, :], past_experts[:, :], float(JT), over_j[:, :],
                                          ALU.mult, ALU.add))
            step(dve.tensor_scalar(over_d[:, :], over_c[:, :], float(CT), float(EX * JT), ALU.add, ALU.min))
            step(dve.tensor_copy(over_column[:, :], over_d[:, :]))
            step(dve.tensor_scalar(over_j[:, :], past_experts[:, :], float(EX - 1), None, ALU.min))
            step(dve.tensor_copy(over_expert[:, :], over_j[:, :]))
            dve.sem_inc(over_ready, 1)

            dve.wait_ge(phase_a_done, 4)

            def x_low(p, i):
                r, j, tt = i // CT, i % CT, p * 2 * CT + i
                dve.wait_ge(xh_made, tt + 1)
                dve.tensor_tensor(xtl[r][:, :, j * P:(j + 1) * P], bank[6 + i % 2].rearrange("p (k n) -> p k n", n=P),
                                  xth[r][:, :, j * P:(j + 1) * P].bitcast(F32), ALU.subtract).then_inc(xl_made, 1)

            def wl_chunk(p, r, n):
                e, m = p * 2 + r, n // NK
                dve.wait_ge(wh_made, (e + 1) * 3 * NK + n + 1)
                w_low(wh[1 - r][:, m, n % NK, :], wl[1 - r][:, m, n % NK, :], raw[:, m, n % NK, :]).then_inc(wl_made, 1)

            def h_low(p, r, l):
                hb = (p * 2 + r) * 2 * NK + l
                w = PARTS[l // NK]
                dve.wait_ge(hh_made, hb + 1)
                dve.tensor_tensor(htl[:, l % NK, w], hm[:, l % 2, 0:w.stop - w.start], hth[:, l % NK, w].bitcast(F32),
                                  ALU.subtract).then_inc(hl_made, 1)

            def gated_product(p, r, l):
                hb = (p * 2 + r) * 2 * NK + l
                dve.wait_ge(silu_made, hb + 3)
                dve.wait_ge(h1_done, hb + 1)
                n = PARTS[l // NK].stop - PARTS[l // NK].start
                dve.tensor_tensor(hm[:, l % 2, 0:n], bank[2 + l % 2][:, 0:n], sl[:, l % 2, 0:n],
                                  ALU.mult).then_inc(hm_made, 1)

            listf = lists.bitcast(F32)

            def finish(p, r, j):
                e = p * 2 + r
                tt = e * CT + j
                dve.wait_ge(out_done, tt + 2)
                dve.wait_ge(acc_loaded[j], (e + 1) * 16)
                dve.scalar_tensor_tensor(acc[:, j, :], bank[4 + (r * CT + j) % 2][:, :],
                                         listf[:, e * JT + j, 1:2], acc[:, j, :],
                                         ALU.mult, ALU.add).then_inc(fin_made, 1)

            def expert(p, r, last):
                nxt = [(p, CT + j) if r == 0 else (p + 1, j) for j in range(CT)]
                for l in range(2 * NK):
                    if l > 0:
                        h_low(p, r, l - 1)
                    if l in (1, 2, 3):
                        x_low(p, r * CT + l + 1)
                    if l in (6, 7) and not last:
                        x_low(*nxt[l - 6])
                    if l >= 2 and not last:
                        wl_chunk(p, r, l - 2)
                    gated_product(p, r, l)
                h_low(p, r, 2 * NK - 1)
                for j in range(CT):
                    if not last:
                        for n in range(2 * NK - 2, 3 * NK)[j + (j > 0):j + 2]:
                            wl_chunk(p, r, n)
                    finish(p, r, j)

            for j in range(FT):
                x_low(0, j)
            dve.wait_ge(lists_loaded, 16)
            with dve.Fori(0, EX // 2 - 1) as p:
                expert(p, 0, False)
                expert(p, 1, False)
            expert(EX // 2 - 1, 0, False)
            expert(EX // 2 - 1, 1, True)

            dve.wait_ge(fin_made, EX * CT + 2)
            over = dve.value_load(tiles_over[0:1, 0:1], min_val=0, max_val=OV)
            with dve.If(over > 0):
                with dve.Fori(0, OV) as k:
                    dve.wait_ge(o_sm, k + 1)
                    dve.wait_ge(o_h01, k + 1)
                    dve.wait_ge(o_copied, k * 3 + 3)
                    dve.tensor_tensor(o_h[:, :], bank[2][:, :], o_s[:, :], ALU.mult).then_inc(o_hm, 1)
                    dve.wait_ge(o_out, k + 1)
                    dve.wait_ge(o_ain, k * 16 + 16)
                    dve.scalar_tensor_tensor(o_r[:, :], bank[4][:, :], o_idx.bitcast(F32)[:, 1:2], o_acc[:, :],
                                             ALU.mult, ALU.add).then_inc(o_fin, 1)

        @block.tensor
        def _(pe):
            pe.wait_ge(ident_made, 2)
            pe.wait_ge(const_made, 2)
            pe.wait_ge(small_loaded, 48)

            def turn_kv(s, c):
                un = s * NC + c
                ch = slice(c * P, (c + 1) * P)
                if c == 0:
                    pe.wait_ge(k_ready, s * GT + GT)
                pe.wait_ge(f2_made, un + 1)
                for j in range(GT):
                    ins = pe.transpose(bank[c % 2][:, j * P:(j + 1) * P], K[:, j, ch], ident[:, :])
                ins.then_inc(k_turned, 1)
                if c == 0:
                    pe.wait_ge(v_loaded, s * 16 + 16)
                pe.wait_ge(vs_made, un + 1)
                for j in range(GT):
                    ins = pe.transpose(bank[2 + c % 2][:, j * P:(j + 1) * P], V[:, j, ch], ident[:, :])
                ins.then_inc(v_turned, 1)

            def turn_y(b, tiles, first_bank=4):
                for j in tiles:
                    if j == 0:
                        pe.wait_ge(y_made, b * NC + NC + 4)
                        pe.wait_ge(first_made, b * NC + NC + 2)
                    if first_bank == 0:
                        if j % 2 == 0:
                            pe.wait_ge((f2_made, vs_made)[j // 2], NG * NC + 2)
                    elif j < 2:
                        pe.wait_ge(xnt_made, b * GT + 1 + j)
                    elif j == 2:
                        pe.wait_ge(ranks_read, b + 1)
                    else:
                        pe.wait_ge(x1_made, b * GT + GT)
                    for c in range(NC):
                        ins = pe.transpose(bank[first_bank + j][:, c * P:(c + 1) * P], Y[:, c, j * P:(j + 1) * P],
                                           ident[:, :])
                    ins.then_inc(y_turned, 1)

            def turn_norm(b, j):
                t = b * GT + j
                pe.wait_ge(xn_made, t + 1)
                pe.wait_ge(xnt_made, t + 1)
                pe.wait_ge(x1_made, b * GT + GT + 4)
                for c in range(NC):
                    ins = pe.transpose(bank[4 + j % 2][:, c * P:(c + 1) * P], XN[:, j, c * P:(c + 1) * P], ident[:, :])
                ins.then_inc(xn_turned, 1)

            def router(b, j, at=0):
                pe.wait_ge(xnt_made, b * GT + j + 3)
                if j in (0, GT // 2) and not at:
                    pe.wait_ge(ranks_read, b + 1)
                for c in range(NC):
                    ins = pe.matmul(logits[at][:, j, :], XNT[:, j % 2, c, :], gk[:, c, :],
                                    start=(c == 0), stop=(c == NC - 1))
                ins.then_inc(gated, 1)

            def rank(k, w=slice(0, GT), at=0):
                pe.wait_ge(mask_made, k + 1)
                pe.matmul(ranks[at][:, w, :], before[:, :], msk[:, w, :], start=True, stop=False)
                for j in range(w.start, w.stop):
                    for i in range(j):
                        pe.matmul(ranks[at][:, j, :], ones[:, :], msk[:, i, :], start=False, stop=False)
                for j in range(w.start, w.stop):
                    ins = pe.matmul(ranks[at][:, j, :], ones[:, :], cum[:, :], start=False, stop=(j == w.stop - 1))
                ins.then_inc(ranked, 1)

            def group(s, back, more):
                b = s - 1
                if back:
                    turn_y(b, (2, 3))
                turn_kv(s, 2)
                turn_kv(s, 3)
                if more:
                    turn_kv(s + 1, 0)
                if back:
                    turn_norm(b, 0)
                    turn_norm(b, 1)
                if more:
                    turn_kv(s + 1, 1)
                if back:
                    router(b, 0)
                    router(b, 1)
                if not more:
                    turn_y(s, range(GT), 0)
                if back:
                    turn_norm(b, 2)
                    turn_norm(b, 3)
                    router(b, 2)
                    router(b, 3)
                if more:
                    turn_y(s, (0, 1))
                if back:
                    rank(b)

            turn_kv(0, 0)
            turn_kv(0, 1)
            group(0, False, True)
            with pe.Fori(1, NG - 1) as s:
                group(s, True, True)
            group(NG - 1, True, False)
            turn_norm(NG - 1, 0)
            for j in range(GT):
                if j + 1 < GT:
                    turn_norm(NG - 1, j + 1)
                router(NG - 1, j, int(j < GT // 2))
                if j == GT // 2:
                    rank(NG - 1, slice(0, GT // 2), 1)
            rank(NG, slice(GT // 2, GT))
            pe.wait_ge(ranks_read, NG + 1)
            pe.matmul(bank[7][:, 128:128 + EX], ones[:, :], cum[:, :], start=True, stop=True).then_inc(totals_made, 1)
            pe.wait_ge(totals_made, 1)
            pe.sem_inc(phase_a_done, 1)

            pe.wait_ge(over_made, 1)

            def turn_x(p, i):
                tt = p * 2 * CT + i
                pe.wait_ge(xg_loaded[i % 2], (p * CT + i // 2 + 1) * 16)
                pe.wait_ge(xl_made, tt + 1)
                for c in range(NK):
                    ins = pe.transpose(bank[6 + i % 2][:, c * P:(c + 1) * P], xg[:, i % 2, c * P:(c + 1) * P],
                                       ident[:, :])
                ins.then_inc(xg_turned, 1)

            def split_product(dst, parts):
                terms = [t for lh_, ll_, rh_, rl_ in parts for t in ((lh_, rh_), (lh_, rl_), (ll_, rh_))]
                for i, (a, b_) in enumerate(terms):
                    ins = pe.matmul(dst, a, b_, start=(i == 0), stop=(i == len(terms) - 1))
                return ins

            def hidden(p, r, l, end=CAP):
                e, half, mb = p * 2 + r, l // NK, l % NK
                hb = e * 2 * NK + l
                w, mc = slice(PARTS[half].start, min(PARTS[half].stop, end)), slice(mb * P, (mb + 1) * P)
                if l == 0:
                    pe.wait_ge(wl_made, e * 3 * NK + NK)
                    pe.wait_ge(xl_made, e * CT + FT + 2)
                if l == NK:
                    pe.wait_ge(xl_made, e * CT + CT + 2)
                for m, free, done in ((0, silu_made, h0_done), (1, hm_made, h1_done)):
                    if l == 0 and m == 1:
                        pe.wait_ge(wl_made, e * 3 * NK + 2 * NK)
                    pe.wait_ge(free, hb + 1)
                    split_product(bank[2 * m + l % 2][:, 0:w.stop - w.start],
                                  [(wh[r][:, m, k, mc], wl[r][:, m, k, mc], xth[r][:, k, w], xtl[r][:, k, w])
                                   for k in range(NK)]).then_inc(done, 1)

            def output(p, r, j):
                e = p * 2 + r
                tw = slice(j * P, (j + 1) * P)
                if j == 0:
                    pe.wait_ge(wl_made, (e + 1) * 3 * NK)
                pe.wait_ge(hl_made, e * 2 * NK + (NK if j < FT else 2 * NK))
                pe.wait_ge(fin_made, e * CT + j + 1)
                split_product(bank[4 + (r * CT + j) % 2][:, :],
                              [(hth[:, k, tw], htl[:, k, tw], wh[r][:, 2, k, :], wl[r][:, 2, k, :])
                               for k in range(NK)]).then_inc(out_done, 1)

            def second_part(p, r, last, end):
                for l in range(NK, 2 * NK):
                    hidden(p, r, l, end)
                    if l in (5, 6) and not last:
                        turn_x(*((p, CT + l - 5) if r == 0 else (p + 1, l - 5)))

            def expert(p, r, last):
                length = pe.value_load(list_length[0:1, bass.ds(p * 2 + r, 1)], min_val=0, max_val=NTOK)
                for l in range(NK):
                    hidden(p, r, l)
                    if l in (0, 1, 2):
                        turn_x(p, r * CT + l + 2)
                with pe.If(length > SHORT):
                    second_part(p, r, last, CAP)
                with pe.Else():
                    with pe.If(length > SHORTER):
                        second_part(p, r, last, SHORT)
                    with pe.Else():
                        second_part(p, r, last, SHORTER)
                for j in range(CT - 1):
                    output(p, r, j)
                with pe.If(length > SHORTER):
                    output(p, r, CT - 1)
                with pe.Else():
                    pe.wait_ge(out_done, (p * 2 + r + 1) * CT)
                    pe.sem_inc(out_done, 1)

            pe.wait_ge(over_ready, 1)
            for j in range(FT):
                turn_x(0, j)
            with pe.Fori(0, EX // 2 - 1) as p:
                expert(p, 0, False)
                expert(p, 1, False)
            expert(EX // 2 - 1, 0, False)
            expert(EX // 2 - 1, 1, True)

            pe.wait_ge(fin_made, EX * CT + 2)
            over = pe.value_load(tiles_over[0:1, 0:1], min_val=0, max_val=OV)
            with pe.If(over > 0):
                with pe.Fori(0, OV) as k:
                    pe.wait_ge(o_xin, k * 16 + 16)
                    for c in range(NK):
                        ins = pe.transpose(bank[6][:, c * P:(c + 1) * P], o_x[:, c * P:(c + 1) * P], ident[:, :])
                    ins.then_inc(o_xturn, 1)
                    pe.wait_ge(o_xtm, k + 1)
                    pe.wait_ge(o_w, k * 48 + 48)
                    for m in range(2):
                        for c in range(NK):
                            ins = pe.matmul(bank[2 * m][:, :], o_xt[:, c, :], raw[:, m, c, :],
                                            start=(c == 0), stop=(c == NK - 1))
                    ins.then_inc(o_h01, 1)
                    pe.wait_ge(o_hm, k + 1)
                    for c in range(NK):
                        ins = pe.transpose(bank[7][:, c * P:(c + 1) * P], o_h[:, c * P:(c + 1) * P], ident[:, :])
                    ins.then_inc(o_hturn, 1)
                    pe.wait_ge(o_htm, k + 1)
                    for c in range(NK):
                        ins = pe.matmul(bank[4][:, :], o_ht[:, c, :], raw[:, 2, c, :],
                                        start=(c == 0), stop=(c == NK - 1))
                    ins.then_inc(o_out, 1)


def kernel(x, ctx_2048, L0_xattn_time_decay, L0_xattn_time_first, L0_ffn_gate_kernel,
           L0_ffn_wi_0, L0_ffn_wi_1, L0_ffn_wo):
    import numpy as np
    import concourse.bacc as bacc
    from concourse.bass_utils import run_bass_kernel_spmd

    nc = bacc.Bacc("TRN2", target_bir_lowering=False, num_devices=1)
    arrays = {
        "in_x": np.ascontiguousarray(x),
        "in_ctx": np.ascontiguousarray(ctx_2048),
        "in_decay": np.ascontiguousarray(np.asarray(L0_xattn_time_decay).reshape(NC, P).T),
        "in_first": np.ascontiguousarray(np.asarray(L0_xattn_time_first).reshape(NC, P).T),
        "in_gate": np.ascontiguousarray(np.asarray(L0_ffn_gate_kernel).reshape(NC, P, EX).transpose(1, 0, 2)),
        "in_wi0": np.ascontiguousarray(L0_ffn_wi_0),
        "in_wi1": np.ascontiguousarray(L0_ffn_wi_1),
        "in_wo": np.ascontiguousarray(L0_ffn_wo),
    }
    args = [nc.dram_tensor(n, a.shape, mybir.dt.from_np(a.dtype), kind="ExternalInput").ap()
            for n, a in arrays.items()]
    out = nc.dram_tensor("out_x", (B, T, C), F32, kind="ExternalOutput").ap()
    build(nc, *args, out)
    r = run_bass_kernel_spmd(nc, [arrays], core_ids=[0])
    return r.results[0]["out_x"]
```
